# Optimizing a Trainium2 kernel written in Bass

```python
import numpy as np
import jax
import jax.numpy as jnp

def _softmax(x, axis=-1):
    return jax.nn.softmax(x, axis=axis)

def _gelu(x):
    return jax.nn.gelu(x, approximate=True)

def _silu(x):
    return jax.nn.silu(x)

def _sigmoid(x):
    return jax.nn.sigmoid(x)

def _layernorm(x, axis=-1, eps=1e-05):
    m = jnp.mean(x, axis=axis, keepdims=True)
    v = jnp.var(x, axis=axis, keepdims=True)
    return (x - m) / jnp.sqrt(v + eps)

def _scatter_add(tgt, idx, src, axis=0):
    return tgt.at[idx].add(src)

def _segment_sum(src, seg, n):
    return jax.ops.segment_sum(src, seg, n)
kernel_name = 'mk_xattn_ffn_d1_seqx_r4_2b9a60'

def setup_inputs(seed: int=0):
    np.random.seed(seed)
    _w = jnp.asarray

    def _rec_inputs():
        import jax
        import jax.numpy as jnp
        _rk = jax.random.key(seed)
        x = -0.0002928 + 1 * jax.random.normal(jax.random.fold_in(_rk, 1), (16, 128, 256), jnp.float32)
        _lenS = 128 - jax.random.randint(jax.random.fold_in(_rk, 7), (16,), 0, max(1, 128 // 4) + 1, jnp.int32)
        _lenS2 = 128 - jax.random.randint(jax.random.fold_in(_rk, 8), (16,), 0, max(1, 128 // 4) + 1, jnp.int32)
        _ctx_1024P = jax.random.normal(jax.random.fold_in(_rk, 11), (16, 16, 256), jnp.float32)
        _ctx_1024c = jax.random.dirichlet(jax.random.fold_in(_rk, 511), 0.3 * jnp.ones((16,), jnp.float32), (16, 128))
        _ctx_1024t = jnp.einsum('bsk,bkd->bsd', _ctx_1024c, _ctx_1024P)
        _ctx_1024t = _ctx_1024t * jax.lax.rsqrt(jnp.mean(jnp.square(_ctx_1024t)) + 1e-12) * 0.953939
        ctx_1024 = -1.39393e-06 + 0.999914 * (_ctx_1024t + 0.3 * jax.random.normal(jax.random.fold_in(_rk, 611), (16, 128, 256), jnp.float32))
        return (x, ctx_1024)
    x, ctx_1024 = _rec_inputs()

    def _L0_xattn_setup():
        import jax, jax.numpy as jnp
        import numpy as np
        B, S, D, NH = (2, 512, 256, 8)
        DH = D // NH
        EPS = 1e-06
        LN_EPS = 1e-05

        def _mlstm_cell(q, k, v, igate_w, igate_b, fgate_w, fgate_b, ln_scale):
            Slen = q.shape[0]
            ifg = jnp.concatenate([q, k, v], axis=-1)
            ig = (ifg @ igate_w.T + igate_b).T
            fg = (ifg @ fgate_w.T + fgate_b).T
            qh = q.reshape(Slen, NH, DH).transpose(1, 0, 2)
            kh = k.reshape(Slen, NH, DH).transpose(1, 0, 2)
            vh = v.reshape(Slen, NH, DH).transpose(1, 0, 2)
            log_f = jax.nn.log_sigmoid(fg)
            cs = jnp.cumsum(log_f, axis=1)
            fg_mat = cs[:, :, None] - cs[:, None, :]
            mask = jnp.tril(jnp.ones((Slen, Slen), dtype=bool))
            log_fg_mat = jnp.where(mask, fg_mat, -jnp.inf)
            log_D = log_fg_mat + ig[:, None, :]
            max_log_D = jnp.max(log_D, axis=-1, keepdims=True)
            D_mat = jnp.exp(log_D - max_log_D)
            qk = jnp.einsum('hsd,htd->hst', qh, kh) / np.sqrt(DH)
            C = qk * D_mat
            normalizer = jnp.maximum(jnp.abs(C.sum(axis=-1, keepdims=True)), jnp.exp(-max_log_D))
            h = jnp.einsum('hst,htd->hsd', C / (normalizer + EPS), vh)
            h = h.transpose(1, 0, 2).reshape(Slen, D)
            mu = h.mean(axis=-1, keepdims=True)
            var = h.var(axis=-1, keepdims=True)
            return (h - mu) / jnp.sqrt(var + LN_EPS) * ln_scale
        key = jax.random.key(seed)
        ks = jax.random.split(key, 8)
        rnd = lambda k, sh, s=1.0: jax.random.normal(k, sh, dtype=jnp.float32) * s
        return {'q': rnd(ks[0], (B, S, D)), 'k': rnd(ks[1], (B, S, D)), 'v': rnd(ks[2], (B, S, D)), 'igate_w': rnd(ks[3], (NH, 3 * D), 0.02), 'igate_b': jnp.linspace(3.0, 6.0, NH, dtype=jnp.float32), 'fgate_w': rnd(ks[4], (NH, 3 * D), 0.02), 'fgate_b': rnd(ks[5], (NH,), 0.3162278), 'ln_scale': jnp.ones((D,), dtype=jnp.float32)}
    _L0_xattn_all = _L0_xattn_setup()
    _L0_xattn_in = {k: v for k, v in _L0_xattn_all.items() if k in ('igate_w', 'igate_b', 'fgate_w', 'fgate_b', 'ln_scale')}
    del _L0_xattn_all

    def _L0_ffn_setup():
        import jax, jax.numpy as jnp
        import numpy as np
        DIM = 256
        DEPTH = 6
        HEADS = 16
        DIM_HEAD = 64
        WINDOW = 64
        INNER = HEADS * DIM_HEAD
        DIM_INNER = int(DIM * 4 * 2 / 3)
        QK_SCALE = 8.0

        def shift_tokens(t):
            a, s = jnp.split(t, 2, -1)
            s = jnp.pad(s, ((0, 0), (1, 0), (0, 0)))[:, :-1]
            return jnp.concatenate([a, s], -1)

        def l2norm(t):
            return t / jnp.maximum(jnp.linalg.norm(t, axis=-1, keepdims=True), 1e-12)

        def rotate_half(x):
            x1, x2 = jnp.split(x, 2, -1)
            return jnp.concatenate([-x2, x1], -1)

        def rotary_tables(n):
            half = jnp.arange(0, DIM_HEAD, 2, dtype=jnp.float32)
            inv_freq = 1.0 / 10000.0 ** (half / DIM_HEAD)
            t = jnp.arange(n, dtype=jnp.float32)
            freqs = t[:, None] * inv_freq[None, :]
            freqs = jnp.concatenate([freqs, freqs], -1)
            base_scale = (half + 0.4 * DIM_HEAD) / (1.4 * DIM_HEAD)
            power = (t - n // 2) / (WINDOW // 2)
            scale = base_scale[None, :] ** power[:, None]
            scale = jnp.concatenate([scale, scale], -1)
            return (freqs, scale)

        def local_attention(q, k, v):
            b, h, n, d = q.shape
            w = WINDOW
            nw = n // w
            bq = q.reshape(b, h, nw, w, d)
            bk = k.reshape(b, h, nw, w, d)
            bv = v.reshape(b, h, nw, w, d)

            def look(t):
                p = jnp.pad(t, ((0, 0), (0, 0), (1, 0), (0, 0), (0, 0)))
                return jnp.concatenate([p[:, :, :nw], p[:, :, 1:]], axis=3)
            bk2, bv2 = (look(bk), look(bv))
            seq = jnp.arange(n).reshape(nw, w)
            seq_p = jnp.pad(seq, ((1, 0), (0, 0)), constant_values=-1)
            jt = jnp.concatenate([seq_p[:nw], seq_p[1:]], axis=1)
            it = seq[:, :, None]
            jb = jt[:, None, :]
            mask = (it < jb) | (it > jb + w) | (jb == -1)
            sim = jnp.einsum('bhwie,bhwje->bhwij', bq, bk2) * QK_SCALE
            sim = jnp.where(mask, -jnp.finfo(sim.dtype).max, sim)
            attn = jax.nn.softmax(sim, -1)
            out = jnp.einsum('bhwij,bhwje->bhwie', attn, bv2)
            return out.reshape(b, h, n, d)

        def attn_layer(x, Wqkv, qs, ksc, Wo):
            b, n, _ = x.shape
            qkv = x @ Wqkv
            q, k, v = jnp.split(qkv, 3, -1)
            sh = lambda t: t.reshape(b, n, HEADS, DIM_HEAD).transpose(0, 2, 1, 3)
            q, k, v = (sh(q), sh(k), sh(v))
            q = l2norm(q) * qs
            k = l2norm(k) * ksc
            freqs, scale = rotary_tables(n)
            cos, sin = (jnp.cos(freqs), jnp.sin(freqs))
            q = q * cos * scale + rotate_half(q) * sin * scale
            inv = 1.0 / scale
            k = k * cos * inv + rotate_half(k) * sin * inv
            out = local_attention(q, k, v)
            out = out.transpose(0, 2, 1, 3).reshape(b, n, INNER)
            return out @ Wo

        def ffn_layer(x, g, bln, W1, b1, W2, b2):
            mu = x.mean(-1, keepdims=True)
            var = ((x - mu) ** 2).mean(-1, keepdims=True)
            xn = (x - mu) / jnp.sqrt(var + 1e-05) * g + bln
            hg = xn @ W1 + b1
            a, gate = jnp.split(hg, 2, -1)
            return a * jax.nn.gelu(gate, approximate=False) @ W2 + b2
        key = jax.random.key(seed)
        ks = jax.random.split(key, 8)
        B, N = (2, 512)
        init = lambda k, shape: jax.random.normal(k, shape, jnp.float32) * 0.02
        return {'x': jax.random.normal(ks[0], (B, N, DIM), jnp.float32), 'Wqkv': init(ks[1], (DEPTH, DIM, 3 * INNER)), 'q_scale': jnp.ones((DEPTH, DIM_HEAD), jnp.float32), 'k_scale': jnp.ones((DEPTH, DIM_HEAD), jnp.float32), 'Wo': init(ks[2], (DEPTH, INNER, DIM)), 'ln_g': jnp.ones((DEPTH, DIM), jnp.float32), 'ln_b': jnp.zeros((DEPTH, DIM), jnp.float32), 'W1': init(ks[3], (DEPTH, DIM, 2 * DIM_INNER)), 'b1': jnp.zeros((DEPTH, 2 * DIM_INNER), jnp.float32), 'W2': init(ks[4], (DEPTH, DIM_INNER, DIM)), 'b2': jnp.zeros((DEPTH, DIM), jnp.float32)}
    _L0_ffn_all = _L0_ffn_setup()
    _L0_ffn_in = {k: v for k, v in _L0_ffn_all.items() if k in ('Wqkv', 'q_scale', 'k_scale', 'Wo', 'ln_g', 'ln_b', 'W1', 'b1', 'W2', 'b2')}
    del _L0_ffn_all
    return {'x': x, 'ctx_1024': ctx_1024, 'L0_xattn_igate_w': _L0_xattn_in['igate_w'], 'L0_xattn_igate_b': _L0_xattn_in['igate_b'], 'L0_xattn_fgate_w': _L0_xattn_in['fgate_w'], 'L0_xattn_fgate_b': _L0_xattn_in['fgate_b'], 'L0_xattn_ln_scale': _L0_xattn_in['ln_scale'], 'L0_ffn_Wqkv': _L0_ffn_in['Wqkv'], 'L0_ffn_q_scale': _L0_ffn_in['q_scale'], 'L0_ffn_k_scale': _L0_ffn_in['k_scale'], 'L0_ffn_Wo': _L0_ffn_in['Wo'], 'L0_ffn_ln_g': _L0_ffn_in['ln_g'], 'L0_ffn_ln_b': _L0_ffn_in['ln_b'], 'L0_ffn_W1': _L0_ffn_in['W1'], 'L0_ffn_b1': _L0_ffn_in['b1'], 'L0_ffn_W2': _L0_ffn_in['W2'], 'L0_ffn_b2': _L0_ffn_in['b2']}

def reference(x, ctx_1024, L0_xattn_igate_w, L0_xattn_igate_b, L0_xattn_fgate_w, L0_xattn_fgate_b, L0_xattn_ln_scale, L0_ffn_Wqkv, L0_ffn_q_scale, L0_ffn_k_scale, L0_ffn_Wo, L0_ffn_ln_g, L0_ffn_ln_b, L0_ffn_W1, L0_ffn_b1, L0_ffn_W2, L0_ffn_b2):
    import jax
    import jax.numpy as jnp

    def _L0_xattn_ref(q, k, v, igate_w, igate_b, fgate_w, fgate_b, ln_scale):
        import jax, jax.numpy as jnp
        import numpy as np
        B, S, D, NH = (2, 512, 256, 8)
        DH = D // NH
        EPS = 1e-06
        LN_EPS = 1e-05

        def _mlstm_cell(q, k, v, igate_w, igate_b, fgate_w, fgate_b, ln_scale):
            Slen = q.shape[0]
            ifg = jnp.concatenate([q, k, v], axis=-1)
            ig = (ifg @ igate_w.T + igate_b).T
            fg = (ifg @ fgate_w.T + fgate_b).T
            qh = q.reshape(Slen, NH, DH).transpose(1, 0, 2)
            kh = k.reshape(Slen, NH, DH).transpose(1, 0, 2)
            vh = v.reshape(Slen, NH, DH).transpose(1, 0, 2)
            log_f = jax.nn.log_sigmoid(fg)
            cs = jnp.cumsum(log_f, axis=1)
            fg_mat = cs[:, :, None] - cs[:, None, :]
            mask = jnp.tril(jnp.ones((Slen, Slen), dtype=bool))
            log_fg_mat = jnp.where(mask, fg_mat, -jnp.inf)
            log_D = log_fg_mat + ig[:, None, :]
            max_log_D = jnp.max(log_D, axis=-1, keepdims=True)
            D_mat = jnp.exp(log_D - max_log_D)
            qk = jnp.einsum('hsd,htd->hst', qh, kh) / np.sqrt(DH)
            C = qk * D_mat
            normalizer = jnp.maximum(jnp.abs(C.sum(axis=-1, keepdims=True)), jnp.exp(-max_log_D))
            h = jnp.einsum('hst,htd->hsd', C / (normalizer + EPS), vh)
            h = h.transpose(1, 0, 2).reshape(Slen, D)
            mu = h.mean(axis=-1, keepdims=True)
            var = h.var(axis=-1, keepdims=True)
            return (h - mu) / jnp.sqrt(var + LN_EPS) * ln_scale
        return jax.vmap(lambda qq, kk, vv: _mlstm_cell(qq, kk, vv, igate_w, igate_b, fgate_w, fgate_b, ln_scale))(q, k, v)

    def _L0_ffn_ref(x, Wqkv, q_scale, k_scale, Wo, ln_g, ln_b, W1, b1, W2, b2):
        import jax, jax.numpy as jnp
        import numpy as np
        DIM = 256
        DEPTH = 6
        HEADS = 16
        DIM_HEAD = 64
        WINDOW = 64
        INNER = HEADS * DIM_HEAD
        DIM_INNER = int(DIM * 4 * 2 / 3)
        QK_SCALE = 8.0

        def shift_tokens(t):
            a, s = jnp.split(t, 2, -1)
            s = jnp.pad(s, ((0, 0), (1, 0), (0, 0)))[:, :-1]
            return jnp.concatenate([a, s], -1)

        def l2norm(t):
            return t / jnp.maximum(jnp.linalg.norm(t, axis=-1, keepdims=True), 1e-12)

        def rotate_half(x):
            x1, x2 = jnp.split(x, 2, -1)
            return jnp.concatenate([-x2, x1], -1)

        def rotary_tables(n):
            half = jnp.arange(0, DIM_HEAD, 2, dtype=jnp.float32)
            inv_freq = 1.0 / 10000.0 ** (half / DIM_HEAD)
            t = jnp.arange(n, dtype=jnp.float32)
            freqs = t[:, None] * inv_freq[None, :]
            freqs = jnp.concatenate([freqs, freqs], -1)
            base_scale = (half + 0.4 * DIM_HEAD) / (1.4 * DIM_HEAD)
            power = (t - n // 2) / (WINDOW // 2)
            scale = base_scale[None, :] ** power[:, None]
            scale = jnp.concatenate([scale, scale], -1)
            return (freqs, scale)

        def local_attention(q, k, v):
            b, h, n, d = q.shape
            w = WINDOW
            nw = n // w
            bq = q.reshape(b, h, nw, w, d)
            bk = k.reshape(b, h, nw, w, d)
            bv = v.reshape(b, h, nw, w, d)

            def look(t):
                p = jnp.pad(t, ((0, 0), (0, 0), (1, 0), (0, 0), (0, 0)))
                return jnp.concatenate([p[:, :, :nw], p[:, :, 1:]], axis=3)
            bk2, bv2 = (look(bk), look(bv))
            seq = jnp.arange(n).reshape(nw, w)
            seq_p = jnp.pad(seq, ((1, 0), (0, 0)), constant_values=-1)
            jt = jnp.concatenate([seq_p[:nw], seq_p[1:]], axis=1)
            it = seq[:, :, None]
            jb = jt[:, None, :]
            mask = (it < jb) | (it > jb + w) | (jb == -1)
            sim = jnp.einsum('bhwie,bhwje->bhwij', bq, bk2) * QK_SCALE
            sim = jnp.where(mask, -jnp.finfo(sim.dtype).max, sim)
            attn = jax.nn.softmax(sim, -1)
            out = jnp.einsum('bhwij,bhwje->bhwie', attn, bv2)
            return out.reshape(b, h, n, d)

        def attn_layer(x, Wqkv, qs, ksc, Wo):
            b, n, _ = x.shape
            qkv = x @ Wqkv
            q, k, v = jnp.split(qkv, 3, -1)
            sh = lambda t: t.reshape(b, n, HEADS, DIM_HEAD).transpose(0, 2, 1, 3)
            q, k, v = (sh(q), sh(k), sh(v))
            q = l2norm(q) * qs
            k = l2norm(k) * ksc
            freqs, scale = rotary_tables(n)
            cos, sin = (jnp.cos(freqs), jnp.sin(freqs))
            q = q * cos * scale + rotate_half(q) * sin * scale
            inv = 1.0 / scale
            k = k * cos * inv + rotate_half(k) * sin * inv
            out = local_attention(q, k, v)
            out = out.transpose(0, 2, 1, 3).reshape(b, n, INNER)
            return out @ Wo

        def ffn_layer(x, g, bln, W1, b1, W2, b2):
            mu = x.mean(-1, keepdims=True)
            var = ((x - mu) ** 2).mean(-1, keepdims=True)
            xn = (x - mu) / jnp.sqrt(var + 1e-05) * g + bln
            hg = xn @ W1 + b1
            a, gate = jnp.split(hg, 2, -1)
            return a * jax.nn.gelu(gate, approximate=False) @ W2 + b2
        for i in range(DEPTH):
            x = attn_layer(shift_tokens(x), Wqkv[i], q_scale[i], k_scale[i], Wo[i]) + x
            x = ffn_layer(shift_tokens(x), ln_g[i], ln_b[i], W1[i], b1[i], W2[i], b2[i]) + x
        return x
    x = x + _L0_xattn_ref(_layernorm(x, axis=-1), ctx_1024, ctx_1024, L0_xattn_igate_w, L0_xattn_igate_b, L0_xattn_fgate_w, L0_xattn_fgate_b, L0_xattn_ln_scale)
    x = x + _L0_ffn_ref(_layernorm(x, axis=-1), L0_ffn_Wqkv, L0_ffn_q_scale, L0_ffn_k_scale, L0_ffn_Wo, L0_ffn_ln_g, L0_ffn_ln_b, L0_ffn_W1, L0_ffn_b1, L0_ffn_W2, L0_ffn_b2)
    return x

_drawn_inputs = setup_inputs


def setup_inputs(seed=0):
    import zlib

    import numpy as np

    out = dict(_drawn_inputs(seed))
    spreads = {'L0_xattn_ln_scale': (1.0, 0.2),
     'L0_ffn_q_scale': (1.0, 0.6),
     'L0_ffn_k_scale': (1.0, 0.6),
     'L0_ffn_ln_g': (1.0, 0.6),
     'L0_ffn_ln_b': (0.0, 0.8),
     'L0_ffn_b1': (0.0, 0.589),
     'L0_ffn_b2': (0.0, 0.1)}
    factors = {}
    for name, (base, spread) in spreads.items():
        noise = np.random.default_rng([zlib.crc32(name.encode()), seed]).standard_normal(out[name].shape)
        drawn = base * np.exp(spread * noise) if base else spread * noise
        out[name] = jnp.asarray(drawn.astype(out[name].dtype))
    for name, factor in factors.items():
        out[name] = (out[name] * factor).astype(out[name].dtype)
    return out
```

```python
from contextlib import ExitStack

import concourse.bass as bass
from concourse import mybir

F32 = mybir.dt.float32
BF16 = mybir.dt.bfloat16
ALU = mybir.AluOpType
ACT = mybir.ActivationFunctionType
AX_X = mybir.AxisListType.X

P = 128
HEADS = 16
DH = 64
HG = 4
GROUPS = HEADS // HG
SLOTS = 2 * GROUPS
QK_SCALE = 8.0
EPS = 1e-5
NORM_FLOOR_SQ = 1e-24
MASKED = -3.0e38
GATE_ROW = 64

C_IDENT, C_SHIFT, C_BAND, C_ROTA, C_ROTB, C_CAUSAL, C_CUMSUM, C_ROWS, C_PICK, C_END = (
    0, 128, 256, 384, 512, 640, 768, 896, 900, 1924)
MH = 8
MD = 32
M_EPS = 1e-6


def live(index, total):
    return not isinstance(index, int) or 0 <= index < total


def due(count):
    return not isinstance(count, int) or count > 0


def program(nc, x, ctxt, gate_w, gate_b, mln_scale, consts, wqk, wv, q_scale, k_scale, wo, ln_g, ln_b, w1, b1, w2, b2, F, out):
    NB, S, D = x.shape
    L = wqk.shape[0]
    NPAIR = NB // 2
    NT = L * NPAIR
    TS = SLOTS * NT
    KC = D // P
    INNER = HEADS * DH
    GF = HG * DH
    OC = INNER // P
    FC = (F + P - 1) // P
    FREM = F - (FC - 1) * P
    fsize = [P] * (FC - 1) + [FREM]
    TOK = 2 * P

    with ExitStack() as ctx:
        def sb(name, shape, dt=F32):
            return ctx.enter_context(nc.sbuf_tensor(name, shape, dt))

        def ps(name):
            return ctx.enter_context(nc.psum_tensor(name, [P, 512], F32))

        def sem(name):
            return ctx.enter_context(nc.semaphore(name))

        pack = sb("pack", [P, C_END])
        ident = pack[:, C_IDENT:C_IDENT + P]
        shift = pack[:, C_SHIFT:C_SHIFT + P]
        rotA = pack[:, C_ROTA:C_ROTA + 2 * DH].rearrange("p (a d) -> p a d", a=2)
        rotB = pack[:, C_ROTB:C_ROTB + 2 * DH].rearrange("p (a d) -> p a d", a=2)
        ident_bf = sb("ident_bf", [P, P], BF16)
        band = pack[:, C_BAND:C_BAND + P].unsqueeze(1).unsqueeze(1).broadcast_to([P, 2, 2, P])
        neghalf = sb("neghalf", [P, 8])
        qk_gain = sb("qk_gain", [P, L, 2, DH])
        lng_col = sb("lng_col", [P, L, KC])
        lnb_col = sb("lnb_col", [P, L, KC])
        b1_col = sb("b1_col", [P, L, 2, FC])
        b2_row = sb("b2_row", [P, L, D])
        Wqk = sb("Wqk", [P, GROUPS, KC, 2 * GF])
        Wv = sb("Wv", [P, GROUPS, KC, GF])
        Wo = sb("Wo", [P, OC, D])
        W1 = sb("W1", [P, 2 * FC - 1, KC, P])
        W2 = sb("W2", [P, FC, D])
        y = sb("y", [P, NB, D])
        x1 = sb("x1", [P, NB, D])

        causal_bf = sb("causal_bf", [P, 4, P], BF16)
        row_scale = pack[:, C_ROWS:C_ROWS + 4]
        cumsum = pack[:, C_CUMSUM:C_CUMSUM + P]
        pick = pack[0:MH, C_PICK:C_PICK + MH * P].rearrange("k (h s) -> k h s", h=MH)
        Wg = sb("Wg", [P, 3 * KC, 2 * MH])
        gbias = sb("gbias", [P, 2 * MH])
        mscale = sb("mscale", [P, D])
        m_bst = sb("m_bst", [P, 6])
        m_mv = sb("m_mv", [P, 2])
        m_ve = sb("m_ve", [P, 1])
        m_rstd = sb("m_rstd", [P, 1])
        qln = [sb(f"qln{i}", [P, D]) for i in range(2)]
        cst = [sb(f"cst{i}", [P, D]) for i in range(2)]
        V33 = [sb(f"V33_{i}", [P, MH, MD + 1]) for i in range(2)]
        qcT = [sb(f"qcT{i}", [P, 2 * KC, P]) for i in range(2)]
        qm = [sb(f"qm{i}", [P, MH, P]) for i in range(2)]
        gts = [sb(f"gts{i}", [P, 2 * MH]) for i in range(2)]
        nf = sb("nf", [P, MH])
        ef = sb("ef", [P, MH])
        lf = sb("lf", [P, MH])
        logf = [sb(f"logf{i}", [P, MH]) for i in range(2)]
        csum = sb("csum", [P, MH])
        gg = sb("gg", [P, MH])
        gT = sb("gT", [MH, P])
        gmax = sb("gmax", [P, MH])
        mlog = sb("mlog", [P, MH])
        dm = sb("dm", [P, MH, P])
        Dm = sb("Dm", [P, MH, P])
        en = [sb(f"en{i}", [P, MH]) for i in range(2)]
        Cm = [sb(f"Cm{i}", [P, MH, P]) for i in range(2)]
        CT = sb("CT", [P, MH, P])
        nrm = sb("nrm", [P, MH])
        nneg = sb("nneg", [P, MH])
        nrm2 = sb("nrm2", [P, MH])
        nrec = sb("nrec", [P, MH])
        hm = sb("hm", [P, D])
        h_bst = sb("h_bst", [P, 6])
        h_mv = sb("h_mv", [P, 2])
        h_ve = sb("h_ve", [P, 1])
        h_rstd = sb("h_rstd", [P, 1])
        hn = sb("hn", [P, D])
        hs = sb("hs", [P, D])
        f_bst = sb("f_bst", [P, 6])
        f_mv = sb("f_mv", [P, 2])
        f_ve = sb("f_ve", [P, 1])
        f_rstd = sb("f_rstd", [P, 1])

        ycur = [sb(f"ycur{i}", [P, D]) for i in range(2)]
        xT = [sb(f"xT{i}", [P, KC, P]) for i in range(2)]
        sq = sb("sq", [P, 2 * GF])
        ss_raw = sb("ss_raw", [P, 8])
        ss = sb("ss", [P, 8])
        rq = sb("rq", [P, 8])
        tabA = sb("tabA", [P, 2, DH])
        tabB = sb("tabB", [P, 2, DH])
        qn = sb("qn", [P, 2 * GF])
        u1 = sb("u1", [P, 2 * GF])
        u2 = sb("u2", [P, 2 * GF])
        u = [sb(f"urot{i}", [P, 2 * GF]) for i in range(2)]
        qkT = [sb(f"qkT{i}", [P, 4, P]) for i in range(2)]
        masked = sb("masked", [P, HG, P])
        mx = sb("mx", [P, HG])
        sc = [sb(f"sc{i}", [P, HG, P]) for i in range(2)]
        pr = [sb(f"pr{i}", [P, HG, P]) for i in range(2)]
        PTs = [sb(f"PTs{i}", [P, HG, P]) for i in range(2)]
        V65 = [sb(f"V65_{i}", [P, HG, DH + 1]) for i in range(4)]
        rec = sb("rec", [P, HG])
        O = [sb(f"O{i}", [P, GF]) for i in range(2)]
        OTs = sb("OTs", [P, OC, P])
        xs = sb("xs", [P, 2, P])
        bst = sb("bst", [P, 2, 2, 6])
        mv = sb("mv", [P, 2, 2])
        ve = sb("ve", [P, 2])
        rstd = sb("rstd", [P, 2])
        wait_carrier = sb("wait_carrier", [P, 1])
        xn = sb("xn", [P, 2, D])
        zT = sb("zT", [P, KC, TOK])
        gel = [sb(f"gel{i}", [P, TOK]) for i in range(2)]
        hT = sb("hT", [P, FC, TOK])
        ffo = sb("ffo", [P, D])

        bQK, bV, bPVO, bPT, bTR, bY = [ps(n) for n in ("bQK", "bV", "bPVO", "bPT", "bTR", "bY")]
        bSIM = ctx.enter_context(nc.psum_tensor("bSIM", [P, 2, 512], F32))
        sims = bSIM[:, :, 0:2 * P].rearrange("p r (i j) -> p r i j", i=2)

        const_in = sem("const_in")
        pool_const = sem("pool_const")
        dve_const = sem("dve_const")
        wqkv_in = [sem(f"wqkv_in{g}") for g in range(GROUPS)]
        wo_in = sem("wo_in")
        w1_in = [sem(f"w1_in{c}") for c in range(FC)]
        w2_in = sem("w2_in")
        out_done = sem("out_done")
        qk_done, v_done, sim_done, pv_done, ot_done, pt_done, tr_done = [
            sem(n) for n in ("qk_done", "v_done", "sim_done", "pv_done", "ot_done", "pt_done", "tr_done")]
        wo_done, w1_done, w2_done, xt_done, sh_done, zt_done = [
            sem(n) for n in ("wo_done", "w1_done", "w2_done", "xt_done", "sh_done", "zt_done")]
        sq_ready, v_ready, exp_ready, ots_ready, pts_ready, qkt_ready = [
            sem(n) for n in ("sq_ready", "v_ready", "exp_ready", "ots_ready", "pts_ready", "qkt_ready")]
        gelu_ready, xts_ready, sh_ready, z_ready = [sem(n) for n in ("gelu_ready", "xts_ready", "sh_ready", "z_ready")]
        ssr_ready, ss_ready, qn_ready, u1_ready, mx_ready, sub_ready, rec_ready, on_ready = [
            sem(n) for n in ("ssr_ready", "ss_ready", "qn_ready", "u1_ready", "mx_ready", "sub_ready", "rec_ready", "on_ready")]
        h_ready, y1_ready, y_ready, ffo_ready, bst_ready, mv_ready, ve_ready, xn_ready = [
            sem(n) for n in ("h_ready", "y1_ready", "y_ready", "ffo_ready", "bst_ready", "mv_ready", "ve_ready", "xn_ready")]
        rq_ready, u2_ready, u_ready, tab_ready, ycur_ready, rstd_ready = [
            sem(n) for n in ("rq_ready", "u2_ready", "u_ready", "tab_ready", "ycur_ready", "rstd_ready")]

        mq_bst, mq_mv, mq_ve, mq_rstd, mq_ready, mc_ready, mT_done, mT_ready, qm_ready = [
            sem(n) for n in ("mq_bst", "mq_mv", "mq_ve", "mq_rstd", "mq_ready", "mc_ready", "mT_done", "mT_ready", "qm_ready")]
        mg_done, gts_ready, nf_ready, ef_ready, lf_ready, logf_ready = [
            sem(n) for n in ("mg_done", "gts_ready", "nf_ready", "ef_ready", "lf_ready", "logf_ready")]
        cs_done, cs_ready, gg_ready, gT_done, gT_ready, mqk_done, gb_done, gmax_ready, dm_ready, mlog_ready = [
            sem(n) for n in ("cs_done", "cs_ready", "gg_ready", "gT_done", "gT_ready", "mqk_done", "gb_done", "gmax_ready",
                             "dm_ready", "mlog_ready")]
        Dm_ready, en_ready, Cm_ready, CT_done, CT_ready, v33_ready, mpv_done = [
            sem(n) for n in ("Dm_ready", "en_ready", "Cm_ready", "CT_done", "CT_ready", "v33_ready", "mpv_done")]
        nrm_ready, nrm2_ready, nrec_ready, hm_ready, mh_bst, mh_mv, mh_ve, mh_rstd, hn_ready, hs_ready = [
            sem(n) for n in ("nrm_ready", "nrm2_ready", "nrec_ready", "hm_ready", "mh_bst", "mh_mv", "mh_ve", "mh_rstd",
                             "hn_ready", "hs_ready")]
        masked_ready = sem("masked_ready")
        nneg_ready = sem("nneg_ready")
        x1_ready, mf_bst, mf_mv, mf_ve, mf_rstd, res_ready = [
            sem(n) for n in ("x1_ready", "mf_bst", "mf_mv", "mf_ve", "mf_rstd", "res_ready")]

        block = ctx.enter_context(nc.Block())

        def m_sweep(eng, step):
            for b in range(4):
                step(b, b % 2)
            with eng.Fori(4, NB - 2, 2) as b:
                step(b, 0)
                step(b + 1, 1)
            for b in range(NB - 2, NB + 2):
                step(b, b % 2)

        def sweep(eng, body):
            body(0)
            body(1)
            with eng.Fori(2, NT) as n:
                body(n)
            body(NT)
            body(NT + 1)

        @block.sync
        def _(sp):
            ld = lambda d, s: sp.dma_start(d, s).then_inc(const_in, 16)
            ld(pack[:], consts)
            ld(Wg[:], gate_w)
            ld(gbias[:], gate_b.broadcast_to([P, 2 * MH]))
            ld(mscale[:], mln_scale.broadcast_to([P, D]))
            ld(x1[:, 0:2], x[0:2].rearrange("b s d -> s b d"))
            ld(y[:, 0:2], ctxt[0:2].rearrange("b s d -> s b d"))
            ld(x1[:, 2:NB], x[2:NB].rearrange("b s d -> s b d"))
            ld(y[:, 2:NB], ctxt[2:NB].rearrange("b s d -> s b d"))
            for l in range(L):
                ld(qk_gain[:, l, 0, :], q_scale[l:l + 1, :].broadcast_to([P, DH]))
                ld(qk_gain[:, l, 1, :], k_scale[l:l + 1, :].broadcast_to([P, DH]))
                ld(b2_row[:, l, :], b2[l:l + 1, :].broadcast_to([P, D]))
            ld(lng_col[:], ln_g)
            ld(lnb_col[:], ln_b)
            ld(b1_col[:], b1)

            def load_layer(l):
                last = SLOTS * NPAIR * l - GROUPS
                for g in range(GROUPS):
                    if due(last + g + 1):
                        sp.wait_ge(v_done, last + g + 1)
                    sp.dma_start(Wqk[:, g], wqk[l, g]).then_inc(wqkv_in[g], 16)
                    sp.dma_start(Wv[:, g], wv[l, g]).then_inc(wqkv_in[g], 16)
                if due(NB * l):
                    sp.wait_ge(wo_done, NB * l)
                sp.dma_start(Wo[:], wo[l]).then_inc(wo_in, 16)
                for c in range(FC):
                    if due(FC * NPAIR * l - FC + c + 1):
                        sp.wait_ge(w1_done, FC * NPAIR * l - FC + c + 1)
                    sp.dma_start(W1[:, 2 * c:min(2 * c + 2, 2 * FC - 1)], w1[l, :, 2 * c:min(2 * c + 2, 2 * FC - 1)]).then_inc(w1_in[c], 16)
                if due(NB * l):
                    sp.wait_ge(w2_done, NB * l)
                sp.dma_start(W2[:], w2[l]).then_inc(w2_in, 16)

            load_layer(0)
            with sp.Fori(1, L) as l:
                load_layer(l)
            for i in range(4):
                sp.wait_ge(res_ready, i + 1)
                q = slice(i * NB // 4, (i + 1) * NB // 4)
                sp.dma_start(out[q].rearrange("b s d -> s b d"), y[:, q, :]).then_inc(out_done, 16)
            sp.wait_ge(out_done, 64)

        n_const = 8 + 3 * L + 3

        @block.tensor
        def _(pe):
            mm = nc.tensor.matmul

            def transpose_y(G, par, s):
                pe.wait_ge(ycur_ready, G + 1)
                if live(s - 3, TS):
                    pe.wait_ge(pts_ready, s - 2)
                for c in range(KC):
                    last = nc.tensor.transpose(bPT[:, c * P:(c + 1) * P], ycur[par][:, c * P:(c + 1) * P], ident)
                last.then_inc(xt_done, 1)

            def body(n):
                layer = n // NPAIR
                for k in range(SLOTS):
                    s = SLOTS * n + k
                    g, half = k % GROUPS, k // GROUPS
                    if live(s, TS):
                        pe.wait_ge(xts_ready, 2 * n + half + 1)
                        pe.wait_ge(wqkv_in[g], 32 * (layer + 1))
                        if due(s):
                            pe.wait_ge(qn_ready, s)
                        for c in range(KC):
                            last = mm(bQK[:], xT[half][:, c, :], Wqk[:, g, c, :], start=c == 0, stop=c == KC - 1)
                        last.then_inc(qk_done, 1)
                    i = s - 3
                    if live(i, TS):
                        pe.wait_ge(exp_ready, i + 1)
                        if due(i):
                            pe.wait_ge(pts_ready, i)
                        if k in (0, 4):
                            G = 2 * n + (1 if k == 4 else 0)
                            if live(G, 2 * NT + 1):
                                pe.wait_ge(xts_ready, G + 1)
                        elif k == 5:
                            if due(n):
                                pe.wait_ge(sh_ready, n)
                        elif k == 6:
                            if due(n):
                                pe.wait_ge(z_ready, n)
                        for h in range(HG):
                            last = nc.tensor.transpose(bPT[:, h * P:(h + 1) * P], pr[(k + 1) % 2][:, h, :], ident)
                        last.then_inc(pt_done, 1)
                    if live(s, TS):
                        if due(s):
                            pe.wait_ge(v_ready, s)
                        if k == 0:
                            if due(2 * n - 1):
                                pe.wait_ge(y1_ready, 2 * n - 1)
                        if k == 4:
                            if due(2 * n):
                                pe.wait_ge(y1_ready, 2 * n)
                        if k == 5:
                            if due(NB + 2 * n - 3):
                                pe.wait_ge(y_ready, NB + 2 * n - 3)
                        if k == 6:
                            if due(NB + 2 * n - 2):
                                pe.wait_ge(y_ready, NB + 2 * n - 2)
                        for c in range(KC):
                            last = mm(bV[:, 0:GF], xT[half][:, c, :], Wv[:, g, c, :], start=c == 0, stop=c == KC - 1)
                        last.then_inc(v_done, 1)
                    i = s - 2
                    if live(i, TS):
                        pe.wait_ge(qkt_ready, i + 1)
                        if due(i):
                            pe.wait_ge(masked_ready, i)
                        for h in range(HG):
                            r0 = DH * (h % 2)
                            last = mm(bSIM[:, h % 2, (h // 2) * P:(h // 2 + 1) * P], qkT[k % 2][r0:r0 + DH, h // 2, :],
                                      qkT[k % 2][r0:r0 + DH, 2 + h // 2, :], start=True, stop=True)
                        last.then_inc(sim_done, 1)
                    i = s - 3
                    if live(i, TS):
                        pe.wait_ge(pts_ready, i + 1)
                        pe.wait_ge(v_ready, i + 1)
                        if due(i):
                            pe.wait_ge(ots_ready, i)
                        for h in range(HG):
                            last = mm(bPVO[:, h * 65:h * 65 + 65], PTs[(k + 1) % 2][:, (h % 2) * 2 + h // 2, :], V65[(k + 1) % 4][:, h, :],
                                      start=True, stop=True)
                        last.then_inc(pv_done, 1)
                    if k in (3, 7):
                        G = 2 * n + (1 if k == 3 else 2)
                        if live(G, 2 * NT + 1):
                            transpose_y(G, 1 if k == 3 else 0, s)
                    if k == 4 and live(n - 1, NT):
                        if due(2 * n):
                            pe.wait_ge(y1_ready, 2 * n)
                        if live(s - 3, TS):
                            pe.wait_ge(pts_ready, s - 2)
                        for b in range(2):
                            bi = (2 * (n - 1) + b) % NB
                            last = mm(bPT[:, b * P:(b + 1) * P], shift, y[:, bi, P:D], start=True, stop=True)
                        last.then_inc(sh_done, 1)
                    if k == 5 and live(n - 1, NT):
                        if due(n):
                            pe.wait_ge(xn_ready, n)
                        if live(s - 3, TS):
                            pe.wait_ge(pts_ready, s - 2)
                        for c in range(KC):
                            for b in range(2):
                                last = nc.tensor.transpose(bPT[:, (2 * c + b) * P:(2 * c + b + 1) * P],
                                                           xn[:, b, c * P:(c + 1) * P], ident)
                        last.then_inc(zt_done, 1)
                    G = 2 * n - 1 if k == 3 else 2 * n
                    if k in (3, 7) and live(G, 2 * NT):
                        pe.wait_ge(ots_ready, 4 * G + 4)
                        pe.wait_ge(wo_in, 16 * (G // NB + 1))
                        if due(s + 1 if live(s, TS) else 0):
                            pe.wait_ge(v_ready, s + 1 if live(s, TS) else 0)
                        for c in range(OC):
                            last = mm(bV[:, 0:D], OTs[:, c, :], Wo[:, c, :], start=c == 0, stop=c == OC - 1)
                        last.then_inc(wo_done, 1)
                    G = 2 * (n - 2) + (k - 4)
                    if k in (4, 5) and live(G, 2 * NT):
                        if due(FC * (n - 1)):
                            pe.wait_ge(h_ready, FC * (n - 1))
                        pe.wait_ge(w2_in, 16 * (G // NB + 1))
                        if live(s, TS):
                            pe.wait_ge(v_ready, s + 1)
                        elif k == 4:
                            if due(min(2 * n, 2 * NT)):
                                pe.wait_ge(y1_ready, min(2 * n, 2 * NT))
                        else:
                            if due(NB + G):
                                pe.wait_ge(y_ready, NB + G)
                        for c in range(FC):
                            last = mm(bV[:, 0:D], hT[0:fsize[c], c, (k - 4) * P:(k - 3) * P], W2[0:fsize[c], c, :],
                                      start=c == 0, stop=c == FC - 1)
                        last.then_inc(w2_done, 1)
                    m, c1 = (n - 1, k - 6) if k >= 6 else (n - 2, k + 2)
                    if k not in (4, 5) and live(m, NT):
                        idx = FC * m + c1
                        if c1 == 0:
                            pe.wait_ge(z_ready, m + 1)
                        pe.wait_ge(w1_in[c1], 16 * (m // NPAIR + 1))
                        if due(idx):
                            pe.wait_ge(h_ready, idx)
                        for a in range(2 if c1 < FC - 1 else 1):
                            for c in range(KC):
                                last = mm(bY[:, a * TOK:(a + 1) * TOK], W1[:, 2 * c1 + a, c, :], zT[:, c, :],
                                          start=c == 0, stop=c == KC - 1)
                        last.then_inc(w1_done, 1)
                    i = s - 3
                    if live(i, TS):
                        pe.wait_ge(on_ready, i + 1)
                        for j in range(2):
                            last = nc.tensor.transpose(bPVO[:, j * P:(j + 1) * P], O[(k + 1) % 2][:, j * P:(j + 1) * P], ident)
                        last.then_inc(ot_done, 1)
                    i = s - 1
                    if live(i, TS):
                        pe.wait_ge(u_ready, i + 1)
                        if due(i):
                            pe.wait_ge(qkt_ready, i)
                        for j in range(4):
                            last = nc.tensor.transpose(bTR[:, j * P:(j + 1) * P], u[(k + 1) % 2][:, j * P:(j + 1) * P], ident)
                        last.then_inc(tr_done, 1)

            def m_step(b, par):
                i = b - 1
                if live(i, NB):
                    pe.wait_ge(logf_ready, i + 1)
                    mm(bY[:, 0:MH], cumsum, logf[1 - par][:], start=True, stop=True).then_inc(cs_done, 1)
                if live(b, NB):
                    pe.wait_ge(mq_ready, b + 1)
                    pe.wait_ge(mc_ready, b + 1)
                    if live(b - 3, NB):
                        if due(b - 2):
                            pe.wait_ge(hm_ready, b - 2)
                    if due(b):
                        pe.wait_ge(qm_ready, b)
                    for a, src in enumerate((qln[par], cst[par])):
                        for c in range(KC):
                            last = nc.tensor.transpose(bQK[:, (a * KC + c) * P:(a * KC + c + 1) * P], src[:, c * P:(c + 1) * P], ident)
                    last.then_inc(mT_done, 1)
                i = b - 1
                if live(i, NB):
                    pe.wait_ge(gg_ready, i + 1)
                    if due(i):
                        pe.wait_ge(gT_ready, i)
                    nc.tensor.transpose(bPVO[0:MH, 0:P], gg[:], ident).then_inc(gT_done, 1)
                if live(b, NB):
                    pe.wait_ge(mT_ready, b + 1)
                    if due(b):
                        pe.wait_ge(gts_ready, b)
                    for c in range(3 * KC):
                        src = qcT[par][:, c if c < 2 * KC else c - KC, :]
                        last = mm(bV[:, 0:2 * MH], src, Wg[:, c, :], start=c == 0, stop=c == 3 * KC - 1)
                    last.then_inc(mg_done, 1)
                i = b - 2
                if live(i, NB):
                    pe.wait_ge(Cm_ready, i + 1)
                    if due(i):
                        pe.wait_ge(CT_ready, i)
                    for h in range(MH):
                        bank = bPT if h < 4 else bTR
                        last = nc.tensor.transpose(bank[:, (h % 4) * P:(h % 4 + 1) * P], Cm[par][:, h, :], ident)
                    last.then_inc(CT_done, 1)
                i = b - 2
                if live(i, NB):
                    pe.wait_ge(CT_ready, i + 1)
                    pe.wait_ge(v33_ready, i + 1)
                    if due(b + 1 if live(b, NB) else 0):
                        pe.wait_ge(qm_ready, b + 1 if live(b, NB) else 0)
                    if due(i):
                        pe.wait_ge(hm_ready, i)
                    for h in range(MH):
                        last = mm(bQK[:, h * (MD + 1):(h + 1) * (MD + 1)], CT[:, h, :], V33[par][:, h, :], start=True, stop=True)
                    last.then_inc(mpv_done, 1)
                i = b - 1
                if live(i, NB):
                    if due(i if live(i - 1, NB) else 0):
                        pe.wait_ge(CT_ready, i if live(i - 1, NB) else 0)
                    pe.wait_ge(qm_ready, i + 1)
                    for h in range(MH):
                        bank = bPT if h < 4 else bTR
                        last = mm(bank[:, (h % 4) * P:(h % 4 + 1) * P], qm[1 - par][:, h, :], qcT[1 - par][:, KC + h // 4, :],
                                  start=True, stop=True)
                    last.then_inc(mqk_done, 1)
                    pe.wait_ge(gT_ready, i + 1)
                    if due(i):
                        pe.wait_ge(dm_ready, i)
                    for r in range(2):
                        mm(bSIM[:, r, :], ident_bf[:], causal_bf[:].rearrange("p h t -> p (h t)"), start=True, stop=False,
                           skip_group_check=True)
                        for h in range(4):
                            last = mm(bSIM[:, r, h * P:(h + 1) * P], pick[:, 4 * r + h, :], gT[:], start=False, stop=h == 3,
                                      skip_group_check=True)
                    last.then_inc(gb_done, 1)

            pe.wait_ge(const_in, 16 * n_const)
            pe.wait_ge(dve_const, 3)
            m_sweep(pe, m_step)
            pe.wait_ge(y_ready, NB)
            transpose_y(0, 0, 0)
            sweep(pe, body)

        @block.scalar
        def _(act):
            fn = nc.scalar.activation

            def evacuate_xT(G, par):
                act.wait_ge(xt_done, G + 1)
                if due(4 * (G - 1)):
                    act.wait_ge(v_done, 4 * (G - 1))
                fn(xT[par][:, 0, :], bPT[:, 0:P], ACT.Copy)
                fn(xT[par][:, 1, 1:P], bPT[:, P:2 * P - 1], ACT.Copy).then_inc(xts_ready, 1)

            def body(n):
                for k in range(SLOTS):
                    s = SLOTS * n + k
                    if live(s, TS):
                        act.wait_ge(qk_done, s + 1)
                        if due(s):
                            act.wait_ge(ssr_ready, s)
                        fn(sq[:], bQK[:], ACT.Square).then_inc(sq_ready, 1)
                    i = s - 3
                    if live(i, TS):
                        act.wait_ge(pt_done, i + 1)
                        if due(i - 1):
                            act.wait_ge(pv_done, i - 1)
                        fn(PTs[(k + 1) % 2][:].rearrange("p h t -> p (h t)"), bPT[:], ACT.Copy).then_inc(pts_ready, 1)
                    if live(s, TS):
                        act.wait_ge(v_done, s + 1)
                        if due(s - 3):
                            act.wait_ge(pv_done, s - 3)
                        fn(V65[k % 4][:, :, 0:DH], bV[:, 0:GF].rearrange("p (h d) -> p h d", h=HG), ACT.Copy).then_inc(v_ready, 1)
                    if k in (3, 7):
                        G = 2 * n + (1 if k == 3 else 2)
                        if live(G, 2 * NT + 1):
                            evacuate_xT(G, 1 if k == 3 else 0)
                    if k == 4 and live(n - 1, NT):
                        if due(n):
                            act.wait_ge(sh_done, n)
                        if due(n - 1):
                            act.wait_ge(xn_ready, n - 1)
                        fn(xs[:].rearrange("p b d -> p (b d)"), bPT[:, 0:TOK], ACT.Copy).then_inc(sh_ready, 1)
                    if k == 5 and live(n - 1, NT):
                        lm = (n - 1) // NPAIR
                        if due(n):
                            act.wait_ge(zt_done, n)
                        if due(FC * (n - 1)):
                            act.wait_ge(w1_done, FC * (n - 1))
                        for c in range(KC):
                            last = fn(zT[:, c, :], bPT[:, c * TOK:(c + 1) * TOK], ACT.Identity,
                                      bias=lnb_col[:, lm, c:c + 1], scale=lng_col[:, lm, c:c + 1])
                        last.then_inc(z_ready, 1)
                    i = s - 2
                    if live(i, TS):
                        act.wait_ge(sub_ready, i + 1)
                        if due(i - 1):
                            act.wait_ge(pt_done, i - 1)
                        fn(pr[k % 2][:], sc[k % 2][:], ACT.Exp).then_inc(exp_ready, 1)
                    m, c1 = (n - 1, k - 6) if k >= 6 else (n - 2, k + 2)
                    if k not in (4, 5) and live(m, NT):
                        idx = FC * m + c1
                        lm = m // NPAIR
                        f = fsize[c1]
                        act.wait_ge(w1_done, idx + 1)
                        if due(idx - 1):
                            act.wait_ge(h_ready, idx - 1)
                        p0, t0 = (0, TOK) if c1 < FC - 1 else (GATE_ROW, 0)
                        fn(gel[c1 % 2][0:f, :], bY[p0:p0 + f, t0:t0 + TOK], ACT.Gelu, bias=b1_col[p0:p0 + f, lm, 1, c1:c1 + 1]).then_inc(gelu_ready, 1)
                    i = s - 3
                    if live(i, TS):
                        act.wait_ge(ot_done, i + 1)
                        if k == 3:
                            if due(2 * n):
                                act.wait_ge(wo_done, 2 * n)
                        if k == 7:
                            if due(2 * n + 1):
                                act.wait_ge(wo_done, 2 * n + 1)
                        g = (k + 1) % 4
                        fn(OTs[:, 2 * g:2 * g + 2, :].rearrange("p c t -> p (c t)"), bPVO[:, 0:GF], ACT.Copy).then_inc(ots_ready, 1)
                    i = s - 1
                    if live(i, TS):
                        act.wait_ge(tr_done, i + 1)
                        if due(i - 1):
                            act.wait_ge(sim_done, i - 1)
                        fn(qkT[(k + 1) % 2][:].rearrange("p c t -> p (c t)"), bTR[:], ACT.Copy).then_inc(qkt_ready, 1)

            def m_step(b, par):
                if live(b, NB):
                    act.wait_ge(mT_done, b + 1)
                    if due(b - 1):
                        act.wait_ge(mqk_done, b - 1)
                    fn(qcT[par][:].rearrange("p c t -> p (c t)"), bQK[:], ACT.Copy).then_inc(mT_ready, 1)
                i = b - 1
                if live(i, NB):
                    act.wait_ge(gT_done, i + 1)
                    if due(i):
                        act.wait_ge(gb_done, i)
                    fn(gT[:], bPVO[0:MH, 0:P], ACT.Copy).then_inc(gT_ready, 1)
                if live(b, NB):
                    act.wait_ge(nf_ready, b + 1)
                    if due(b):
                        act.wait_ge(lf_ready, b)
                    fn(ef[:], nf[:], ACT.Exp).then_inc(ef_ready, 1)
                    act.wait_ge(ef_ready, b + 1)
                    if due(b):
                        act.wait_ge(logf_ready, b)
                    fn(lf[:], ef[:], ACT.Ln, bias=1.0).then_inc(lf_ready, 1)
                i = b - 2
                if live(i, NB):
                    act.wait_ge(CT_done, i + 1)
                    if due(i):
                        act.wait_ge(mpv_done, i)
                    fn(CT[:, 0:4].rearrange("p h t -> p (h t)"), bPT[:], ACT.Copy)
                    fn(CT[:, 4:8].rearrange("p h t -> p (h t)"), bTR[:], ACT.Copy).then_inc(CT_ready, 1)
                i = b - 1
                if live(i, NB):
                    act.wait_ge(dm_ready, i + 1)
                    if due(i):
                        act.wait_ge(Cm_ready, i)
                    fn(Dm[:], dm[:], ACT.Exp).then_inc(Dm_ready, 1)
                    act.wait_ge(mlog_ready, i + 1)
                    if due(i - 1):
                        act.wait_ge(nrm_ready, i - 1)
                    fn(en[1 - par][:], mlog[:], ACT.Exp, scale=-1.0).then_inc(en_ready, 1)
                if live(b, NB):
                    act.wait_ge(mc_ready, b + 1)
                    if due(b - 1):
                        act.wait_ge(mpv_done, b - 1)
                    fn(V33[par][:, :, 0:MD], cst[par][:].rearrange("p (h d) -> p h d", h=MH), ACT.Copy).then_inc(v33_ready, 1)

            act.wait_ge(dve_const, 3)
            m_sweep(act, m_step)
            evacuate_xT(0, 0)
            sweep(act, body)

        @block.vector
        def _(dve):
            V = nc.vector

            def residual(G):
                dve.wait_ge(wo_done, G + 1)
                dve.wait_ge(y_ready, G + 1)
                b = G % NB
                V.tensor_tensor(y[:, b, :], y[:, b, :], bV[:, 0:D], ALU.add).then_inc(y1_ready, 1)

            def final_add(G):
                b, lm = G % NB, G // NB
                dve.wait_ge(w2_done, G + 1)
                V.tensor_tensor(ffo[:], bV[:, 0:D], b2_row[:, lm, :], ALU.add).then_inc(ffo_ready, 1)
                dve.wait_ge(ffo_ready, G + 1)
                V.tensor_tensor(y[:, b, :], y[:, b, :], ffo[:], ALU.add).then_inc(y_ready, 1)

            def body(n):
                for k in range(SLOTS):
                    s = SLOTS * n + k
                    if live(s, TS):
                        dve.wait_ge(sq_ready, s + 1)
                        if due(s):
                            dve.wait_ge(ss_ready, s)
                        V.tensor_reduce(ss_raw[:], sq[:].rearrange("p (h d) -> p h d", d=DH), axis=AX_X, op=ALU.add).then_inc(ssr_ready, 1)
                        dve.wait_ge(ssr_ready, s + 1)
                        if due(s):
                            dve.wait_ge(rq_ready, s)
                        V.tensor_scalar_max(ss[:], ss_raw[:], NORM_FLOOR_SQ).then_inc(ss_ready, 1)
                    if k == 5 and live(n - 1, NT):
                        if due(n):
                            dve.wait_ge(rstd_ready, n)
                        if due(n - 1):
                            dve.wait_ge(zt_done, n - 1)
                        for b in range(2):
                            bi = (2 * (n - 1) + b) % NB
                            V.tensor_scalar(xn[:, b, 0:P], y[:, bi, 0:P], mv[:, b, 0:1], rstd[:, b:b + 1], ALU.subtract, ALU.mult)
                            last = V.tensor_scalar(xn[:, b, P:D], xs[:, b, :], mv[:, b, 0:1], rstd[:, b:b + 1], ALU.subtract, ALU.mult)
                        last.then_inc(xn_ready, 1)
                    i = s - 2
                    if live(i, TS):
                        dve.wait_ge(sim_done, i + 1)
                        if due(i):
                            dve.wait_ge(sub_ready, i)
                        V.tensor_tensor(masked[:].rearrange("p (r i) j -> p r i j", r=2), sims, band, ALU.add).then_inc(masked_ready, 1)
                        dve.wait_ge(masked_ready, i + 1)
                        V.tensor_reduce(mx[:], masked[:], axis=AX_X, op=ALU.max).then_inc(mx_ready, 1)
                    i = s - 3
                    if live(i, TS):
                        pv = bPVO[:, 0:HG * 65].rearrange("p (h d) -> p h d", h=HG)
                        dve.wait_ge(pv_done, i + 1)
                        if due(i):
                            dve.wait_ge(on_ready, i)
                        V.reciprocal(rec[:].unsqueeze(2), pv[:, :, DH:DH + 1]).then_inc(rec_ready, 1)
                        dve.wait_ge(rec_ready, i + 1)
                        if due(i - 1):
                            dve.wait_ge(ot_done, i - 1)
                        V.tensor_tensor(O[(k + 1) % 2][:].rearrange("p (h d) -> p h d", h=HG), pv[:, :, 0:DH],
                                        rec[:].unsqueeze(2).broadcast_to([P, HG, DH]), ALU.mult).then_inc(on_ready, 1)
                    i = s - 2
                    if live(i, TS):
                        dve.wait_ge(mx_ready, i + 1)
                        if due(i - 1):
                            dve.wait_ge(exp_ready, i - 1)
                        V.tensor_tensor(sc[k % 2][:], masked[:], mx[:].unsqueeze(2).broadcast_to([P, HG, P]),
                                        ALU.subtract).then_inc(sub_ready, 1)
                    if live(s, TS):
                        dve.wait_ge(rq_ready, s + 1)
                        if due(s):
                            dve.wait_ge(u_ready, s)
                        V.tensor_tensor(qn[:].rearrange("p (h d) -> p h d", d=DH), bQK[:].rearrange("p (h d) -> p h d", d=DH),
                                        rq[:].unsqueeze(2).broadcast_to([P, 2 * HG, DH]), ALU.mult).then_inc(qn_ready, 1)
                        dve.wait_ge(qn_ready, s + 1)
                        dve.wait_ge(tab_ready, n + 1)
                        V.tensor_tensor(u1[:].rearrange("p (a h d) -> p a h d", a=2, h=HG), qn[:].rearrange("p (a h d) -> p a h d", a=2, h=HG),
                                        tabA[:].unsqueeze(2).broadcast_to([P, 2, HG, DH]), ALU.mult).then_inc(u1_ready, 1)
                    if k == 3 and live(2 * n - 1, 2 * NT):
                        residual(2 * n - 1)
                    if k == 7 and live(2 * n, 2 * NT):
                        residual(2 * n)
                    if k == 4 and live(n - 1, NT):
                        if due(n):
                            dve.wait_ge(sh_ready, n)
                        if due(2 * n):
                            dve.wait_ge(y1_ready, 2 * n)
                        if due(n - 1):
                            dve.wait_ge(mv_ready, n - 1)
                        for b in range(2):
                            bi = (2 * (n - 1) + b) % NB
                            V.bn_stats(bst[:, b, 0, :], y[:, bi, 0:P])
                            last = V.bn_stats(bst[:, b, 1, :], xs[:, b, :])
                        last.then_inc(bst_ready, 1)
                        if due(n):
                            dve.wait_ge(bst_ready, n)
                        if due(n - 1):
                            dve.wait_ge(xn_ready, n - 1)
                        V.memset(wait_carrier[:], 0.0)
                        V.bn_aggr(mv[:, 0, :], bst[:, 0].rearrange("p a b -> p (a b)"))
                        V.bn_aggr(mv[:, 1, :], bst[:, 1].rearrange("p a b -> p (a b)")).then_inc(mv_ready, 1)
                        if due(n):
                            dve.wait_ge(mv_ready, n)
                        if due(n - 1):
                            dve.wait_ge(rstd_ready, n - 1)
                        V.tensor_scalar_add(ve[:], mv[:, :, 1], EPS).then_inc(ve_ready, 1)
                    G = 2 * (n - 2) + (k - 4)
                    if k in (4, 5) and live(G, 2 * NT):
                        final_add(G)
                    m, c1 = (n - 1, k - 6) if k >= 6 else (n - 2, k + 2)
                    if k not in (4, 5) and live(m, NT):
                        idx = FC * m + c1
                        lm = m // NPAIR
                        f = fsize[c1]
                        dve.wait_ge(gelu_ready, idx + 1)
                        if c1 == 0:
                            if due(2 * m):
                                dve.wait_ge(w2_done, 2 * m)
                        V.scalar_tensor_tensor(hT[0:f, c1, :], bY[0:f, 0:TOK], b1_col[0:f, lm, 0, c1:c1 + 1], gel[c1 % 2][0:f, :],
                                               op0=ALU.add, op1=ALU.mult).then_inc(h_ready, 1)

            dve.wait_ge(const_in, 16 * n_const)
            V.tensor_copy(ident_bf[:], ident).then_inc(dve_const, 1)
            for i in range(2):
                V.memset(xT[i][:, 1, 0:1], 0.0)
            for i in range(4):
                last = V.memset(V65[i][:, :, DH:DH + 1], 1.0)
            last.then_inc(dve_const, 1)
            V.tensor_copy(causal_bf[:], pack[:, C_CAUSAL:C_CAUSAL + P].unsqueeze(1).broadcast_to([P, 4, P]))
            for i in range(2):
                V.memset(V33[i][:, :, MD:MD + 1], 1.0)
            V.memset(neghalf[:], -0.5).then_inc(dve_const, 1)

            def statistics(src, bst_, mv_, ve_, s_bst, s_mv, s_ve, count, freed):
                if due(freed[1]):
                    dve.wait_ge(freed[0], freed[1])
                V.memset(wait_carrier[:], 0.0)
                V.bn_stats(bst_[:], src).then_inc(s_bst, 1)
                dve.wait_ge(s_bst, count)
                V.memset(wait_carrier[:], 0.0)
                V.bn_aggr(mv_[:], bst_[:]).then_inc(s_mv, 1)
                dve.wait_ge(s_mv, count)
                V.tensor_scalar_add(ve_[:], mv_[:, 1:2], EPS).then_inc(s_ve, 1)

            def query_statistics(b):
                statistics(x1[:, b, :], m_bst, m_mv, m_ve, mq_bst, mq_mv, mq_ve, b + 1, (mq_ready, b))

            def query(b, par):
                dve.wait_ge(mq_rstd, b + 1)
                if due(b - 1):
                    dve.wait_ge(mT_done, b - 1)
                V.tensor_scalar(qln[par][:], x1[:, b, :], m_mv[:, 0:1], m_rstd[:, 0:1], ALU.subtract, ALU.mult).then_inc(mq_ready, 1)

            def m_step(b, par):
                i = b - 1
                if live(i, NB):
                    dve.wait_ge(cs_done, i + 1)
                    if due(i):
                        dve.wait_ge(mlog_ready, i)
                    if due(i):
                        dve.wait_ge(gT_done, i)
                    V.tensor_tensor(gg[:], gts[1 - par][:, 0:MH], bY[:, 0:MH], ALU.subtract).then_inc(gg_ready, 1)
                    V.tensor_copy(csum[:], bY[:, 0:MH]).then_inc(cs_ready, 1)
                i = b - 2
                if live(i, NB):
                    dve.wait_ge(Dm_ready, i + 1)
                    dve.wait_ge(mqk_done, i + 1)
                    if due(i - 1):
                        dve.wait_ge(CT_done, i - 1)
                    V.tensor_tensor(Cm[par][:, 0:4].rearrange("p h t -> p (h t)"), bPT[:], Dm[:, 0:4].rearrange("p h t -> p (h t)"), ALU.mult)
                    V.tensor_tensor(Cm[par][:, 4:8].rearrange("p h t -> p (h t)"), bTR[:], Dm[:, 4:8].rearrange("p h t -> p (h t)"), ALU.mult).then_inc(Cm_ready, 1)
                if live(b, NB):
                    dve.wait_ge(mT_ready, b + 1)
                    if due(b - 1):
                        dve.wait_ge(mqk_done, b - 1)
                    for c in range(KC):
                        last = V.tensor_tensor(qm[par][:, 4 * c:4 * c + 4, :], bQK[:, c * P:(c + 1) * P].unsqueeze(1).broadcast_to([P, 4, P]),
                                               row_scale.unsqueeze(2).broadcast_to([P, 4, P]), ALU.mult)
                    last.then_inc(qm_ready, 1)
                    dve.wait_ge(mg_done, b + 1)
                    if due(b - 1):
                        dve.wait_ge(gg_ready, b - 1)
                    V.tensor_tensor(gts[par][:], bV[:, 0:2 * MH], gbias[:], ALU.add).then_inc(gts_ready, 1)
                    fg = gts[par][:, MH:2 * MH]
                    dve.wait_ge(gts_ready, b + 1)
                    if due(b):
                        dve.wait_ge(ef_ready, b)
                    V.scalar_tensor_tensor(nf[:], fg, -1.0, fg, op0=ALU.mult, op1=ALU.min).then_inc(nf_ready, 1)
                    dve.wait_ge(lf_ready, b + 1)
                    if due(b - 1):
                        dve.wait_ge(cs_done, b - 1)
                    V.scalar_tensor_tensor(logf[par][:], fg, 0.0, lf[:], op0=ALU.min, op1=ALU.subtract).then_inc(logf_ready, 1)
                i = b - 2
                if live(i, NB):
                    hv = bQK[:, 0:MH * (MD + 1)].rearrange("p (h d) -> p h d", h=MH)
                    dve.wait_ge(mpv_done, i + 1)
                    dve.wait_ge(en_ready, i + 1)
                    V.scalar_tensor_tensor(nneg[:].unsqueeze(2), hv[:, :, MD:MD + 1], -1.0, en[par][:].unsqueeze(2),
                                           op0=ALU.mult, op1=ALU.max).then_inc(nneg_ready, 1)
                    dve.wait_ge(nneg_ready, i + 1)
                    V.tensor_tensor(nrm[:].unsqueeze(2), hv[:, :, MD:MD + 1], nneg[:].unsqueeze(2), ALU.max).then_inc(nrm_ready, 1)
                    dve.wait_ge(nrm_ready, i + 1)
                    V.tensor_scalar_add(nrm2[:], nrm[:], M_EPS).then_inc(nrm2_ready, 1)
                    dve.wait_ge(nrm2_ready, i + 1)
                    if due(i):
                        dve.wait_ge(hm_ready, i)
                    V.reciprocal(nrec[:], nrm2[:]).then_inc(nrec_ready, 1)
                    dve.wait_ge(nrec_ready, i + 1)
                    if due(i):
                        dve.wait_ge(hn_ready, i)
                    V.tensor_tensor(hm[:].rearrange("p (h d) -> p h d", h=MH), hv[:, :, 0:MD],
                                    nrec[:].unsqueeze(2).broadcast_to([P, MH, MD]), ALU.mult).then_inc(hm_ready, 1)
                    dve.wait_ge(hm_ready, i + 1)
                    statistics(hm[:], h_bst, h_mv, h_ve, mh_bst, mh_mv, mh_ve, i + 1, (mh_rstd, i))
                if live(b + 1, NB):
                    query_statistics(b + 1)
                i = b - 2
                if live(i, NB):
                    dve.wait_ge(mh_rstd, i + 1)
                    V.tensor_scalar(hn[:], hm[:], h_mv[:, 0:1], h_rstd[:, 0:1], ALU.subtract, ALU.mult).then_inc(hn_ready, 1)
                    dve.wait_ge(hn_ready, i + 1)
                    V.tensor_tensor(hs[:], hn[:], mscale[:], ALU.mult).then_inc(hs_ready, 1)
                    dve.wait_ge(hs_ready, i + 1)
                    V.tensor_tensor(x1[:, i, :], x1[:, i, :], hs[:], ALU.add).then_inc(x1_ready, 1)
                if live(b + 1, NB):
                    query(b + 1, 1 - par)
                i = b - 2
                if live(i, NB):
                    dve.wait_ge(x1_ready, i + 1)
                    statistics(x1[:, i, :], f_bst, f_mv, f_ve, mf_bst, mf_mv, mf_ve, i + 1, (y_ready, i))
                i = b - 1
                if live(i, NB):
                    bands = bSIM[:].rearrange("p r (h t) -> p (r h) t", h=4)
                    dve.wait_ge(gb_done, i + 1)
                    if due(i):
                        dve.wait_ge(dm_ready, i)
                    V.tensor_reduce(gmax[:], bands, axis=AX_X, op=ALU.max).then_inc(gmax_ready, 1)
                    dve.wait_ge(gmax_ready, i + 1)
                    if due(i):
                        dve.wait_ge(Dm_ready, i)
                    V.tensor_tensor(dm[:], bands, gmax[:].unsqueeze(2).broadcast_to([P, MH, P]), ALU.subtract).then_inc(dm_ready, 1)
                    dve.wait_ge(cs_ready, i + 1)
                    if due(i):
                        dve.wait_ge(en_ready, i)
                    V.tensor_tensor(mlog[:], csum[:], gmax[:], ALU.add).then_inc(mlog_ready, 1)
                i = b - 2
                if live(i, NB):
                    dve.wait_ge(mf_rstd, i + 1)
                    V.tensor_scalar(y[:, i, :], x1[:, i, :], f_mv[:, 0:1], f_rstd[:, 0:1], ALU.subtract, ALU.mult).then_inc(y_ready, 1)

            query_statistics(0)
            query(0, 0)
            m_sweep(dve, m_step)
            sweep(dve, body)
            for i in range(4):
                q = slice(i * NB // 4, (i + 1) * NB // 4)
                dve.wait_ge(y_ready, NB * L + (i + 1) * NB // 4)
                V.tensor_tensor(y[:, q, :], y[:, q, :], x1[:, q, :], ALU.add).then_inc(res_ready, 1)

        @block.gpsimd
        def _(pool):
            T = nc.gpsimd.tensor_tensor

            def stage_y(G, par):
                pool.wait_ge(y_ready, G + 1)
                if due(G - 1):
                    pool.wait_ge(xt_done, G - 1)
                nc.gpsimd.tensor_copy(ycur[par][:], y[:, G % NB, :]).then_inc(ycur_ready, 1)

            def body(n):
                for k in range(SLOTS):
                    s = SLOTS * n + k
                    if k == 0 and live(n, NT):
                        layer = n // NPAIR
                        if due(SLOTS * n):
                            pool.wait_ge(u_ready, SLOTS * n)
                        gain = qk_gain[:, layer]
                        T(tabA[:], rotA, gain, ALU.mult)
                        T(tabB[:, :, 0:DH // 2], rotB[:, :, 0:DH // 2], gain[:, :, DH // 2:DH], ALU.mult)
                        T(tabB[:, :, DH // 2:DH], rotB[:, :, DH // 2:DH], gain[:, :, 0:DH // 2], ALU.mult).then_inc(tab_ready, 1)
                    if live(s, TS):
                        pool.wait_ge(ss_ready, s + 1)
                        if due(s):
                            pool.wait_ge(qn_ready, s)
                        T(rq[:], ss[:], neghalf[:], ALU.pow).then_inc(rq_ready, 1)
                        pool.wait_ge(qn_ready, s + 1)
                        pool.wait_ge(tab_ready, n + 1)
                        if due(s):
                            pool.wait_ge(u_ready, s)
                        for a in range(2):
                            src = qn[:, a * GF:(a + 1) * GF].rearrange("p (h d) -> p h d", h=HG)
                            dst = u2[:, a * GF:(a + 1) * GF].rearrange("p (h d) -> p h d", h=HG)
                            for lo, hi in ((0, DH // 2), (DH // 2, 0)):
                                last = T(dst[:, :, lo:lo + DH // 2], src[:, :, hi:hi + DH // 2],
                                         tabB[:, a:a + 1, lo:lo + DH // 2].broadcast_to([P, HG, DH // 2]), ALU.mult)
                        last.then_inc(u2_ready, 1)
                        pool.wait_ge(u2_ready, s + 1)
                        pool.wait_ge(u1_ready, s + 1)
                        if due(s - 1):
                            pool.wait_ge(tr_done, s - 1)
                        T(u[k % 2][:], u1[:], u2[:], ALU.add).then_inc(u_ready, 1)
                    if k in (2, 6):
                        G = 2 * n + (1 if k == 2 else 2)
                        if live(G, 2 * NT + 1):
                            stage_y(G, 1 if k == 2 else 0)
                    if k == 4 and live(n - 1, NT):
                        if due(n):
                            pool.wait_ge(ve_ready, n)
                        if due(n - 1):
                            pool.wait_ge(xn_ready, n - 1)
                        T(rstd[:], ve[:], neghalf[:, 0:2], ALU.pow).then_inc(rstd_ready, 1)

            pool.wait_ge(const_in, 16 * n_const)
            pool.wait_ge(dve_const, 3)

            def inverse_root(ve_, rstd_, s_ve, s_rstd, count, used):
                pool.wait_ge(s_ve, count)
                if due(count - 1):
                    pool.wait_ge(used, count - 1)
                T(rstd_[:], ve_[:], neghalf[:, 0:1], ALU.pow).then_inc(s_rstd, 1)

            def context_copy(b, par):
                if due(b - 1):
                    pool.wait_ge(mT_done, b - 1)
                if due(b - 1):
                    pool.wait_ge(v33_ready, b - 1)
                nc.gpsimd.tensor_copy(cst[par][:], y[:, b, :]).then_inc(mc_ready, 1)

            def m_step(b, par):
                if live(b + 1, NB):
                    context_copy(b + 1, 1 - par)
                i = b - 2
                if live(i, NB):
                    inverse_root(h_ve, h_rstd, mh_ve, mh_rstd, i + 1, hn_ready)
                if live(b + 1, NB):
                    inverse_root(m_ve, m_rstd, mq_ve, mq_rstd, b + 2, mq_ready)
                if live(i, NB):
                    inverse_root(f_ve, f_rstd, mf_ve, mf_rstd, i + 1, y_ready)

            inverse_root(m_ve, m_rstd, mq_ve, mq_rstd, 1, mq_ready)
            context_copy(0, 0)
            m_sweep(pool, m_step)
            stage_y(0, 0)
            sweep(pool, body)


def constants(S, D):
    import numpy as np
    f = np.float32
    t = np.arange(S, dtype=f)
    half = np.arange(0, DH, 2, dtype=f)
    inv_freq = (f(1.0) / f(10000.0) ** (half / f(DH))).astype(f)
    freqs = np.concatenate([t[:, None] * inv_freq[None, :]] * 2, -1).astype(f)
    base = (half + f(0.4 * DH)) / f(1.4 * DH)
    power = (t - S // 2) / f(DH // 2)
    scale = np.concatenate([(base[None, :] ** power[:, None])] * 2, -1).astype(f)
    cos, sin = np.cos(freqs), np.sin(freqs)
    sign = np.concatenate([-np.ones(DH // 2), np.ones(DH // 2)]).astype(f)
    i, j = np.arange(S)[:, None], np.arange(S)[None, :]
    pack = np.zeros((S, C_END), f)
    pack[:, C_IDENT:C_IDENT + S] = i == j
    pack[:, C_SHIFT:C_SHIFT + S] = j == i + 1
    pack[:, C_BAND:C_BAND + S] = np.where((j <= i) & (i <= j + DH), f(0), f(MASKED))
    pack[:, C_CAUSAL:C_CAUSAL + S] = np.where(j <= i, f(0), f(MASKED))
    pack[:, C_CUMSUM:C_CUMSUM + S] = i <= j
    for h in range(4):
        pack[MD * h:MD * (h + 1), C_ROWS + h] = f(1.0) / np.sqrt(f(MD))
    for h in range(MH):
        pack[h, C_PICK + h * P:C_PICK + (h + 1) * P] = 1
    pack[:, C_ROTA:C_ROTA + 2 * DH] = np.concatenate([cos * scale * f(QK_SCALE), cos / scale], 1)
    pack[:, C_ROTB:C_ROTB + 2 * DH] = np.concatenate([sin * sign * scale * f(QK_SCALE), sin * sign / scale], 1)
    return pack


def lay_out(w):
    import numpy as np
    a = {k: np.ascontiguousarray(v) for k, v in w.items()}
    L, D, _ = a['Wqkv'].shape
    kc, inner, gf = D // P, HEADS * DH, HG * DH
    f = a['W2'].shape[1]
    fc = -(-f // P)
    qkv = a['Wqkv'].reshape(L, kc, P, 3, GROUPS, gf)
    qk = qkv[:, :, :, 0:2].transpose(0, 4, 2, 1, 3, 5).reshape(L, GROUPS, P, kc, 2 * gf)
    v = qkv[:, :, :, 2].transpose(0, 3, 2, 1, 4)
    wo = a['Wo'].reshape(L, inner // P, P, D).transpose(0, 2, 1, 3)
    whole = (fc - 1) * P
    w1 = np.zeros((L, D, 2 * fc - 1, P), a['W1'].dtype)
    halves = a['W1'].reshape(L, D, 2, f)
    w1[:, :, 0:2 * fc - 2] = halves[:, :, :, 0:whole].reshape(L, D, 2, fc - 1, P).transpose(0, 1, 3, 2, 4).reshape(L, D, 2 * fc - 2, P)
    w1[:, :, 2 * fc - 2, 0:f - whole] = halves[:, :, 0, whole:]
    w1[:, :, 2 * fc - 2, GATE_ROW:GATE_ROW + f - whole] = halves[:, :, 1, whole:]
    w1 = w1.reshape(L, kc, P, 2 * fc - 1, P).transpose(0, 2, 3, 1, 4)
    w2 = np.zeros((L, fc * P, D), a['W2'].dtype)
    w2[:, 0:f] = a['W2']
    w2 = w2.reshape(L, fc, P, D).transpose(0, 2, 1, 3)
    b1 = np.zeros((L, 2, fc * P), a['b1'].dtype)
    b1[:, :, 0:f] = a['b1'].reshape(L, 2, f)
    b1[:, 1, whole + GATE_ROW:whole + GATE_ROW + f - whole] = b1[:, 1, whole:f].copy()
    b1 = b1.reshape(L, 2, fc, P).transpose(3, 0, 1, 2)
    gates = np.stack([a['igate_w'], a['fgate_w']]).reshape(2 * MH, 3 * kc, P).transpose(2, 1, 0)
    gate_b = np.stack([a['igate_b'], a['fgate_b']]).reshape(1, 2 * MH)
    g, b = (a[k].reshape(L, kc, P).transpose(2, 0, 1) for k in ('ln_g', 'ln_b'))
    return dict(gate_w=gates, gate_b=gate_b, mln_scale=a['ln_scale'].reshape(1, D), wqk=qk, wv=v, q_scale=a['q_scale'], k_scale=a['k_scale'], wo=wo, ln_g=g, ln_b=b, w1=w1, b1=b1, w2=w2,
                b2=a['b2'])


def kernel(**inputs):
    import numpy as _np
    import concourse.bacc as _bacc
    from concourse import mybir as _mybir
    from concourse.bass_utils import run_bass_kernel_spmd as _run

    nc = _bacc.Bacc("TRN2", target_bir_lowering=False, num_devices=1)
    arrays, args = {}, {}
    x = inputs['x']
    w = dict(x=x, ctxt=inputs['ctx_1024'], consts=constants(*x.shape[1:]))
    w.update(lay_out({k.split('_', 2)[2]: v for k, v in inputs.items() if k.startswith('L0_')}))
    for name, a in w.items():
        a = _np.ascontiguousarray(a)
        arrays[f"in_{name}_dram"] = a
        args[name] = nc.dram_tensor(f"in_{name}_dram", a.shape, _mybir.dt.from_np(a.dtype), kind="ExternalInput").ap()
    shape = x.shape
    out = nc.dram_tensor("out_dram", shape, _mybir.dt.float32, kind="ExternalOutput").ap()
    program(nc, args['x'], args['ctxt'], args['gate_w'], args['gate_b'], args['mln_scale'], args['consts'], args['wqk'], args['wv'], args['q_scale'], args['k_scale'], args['wo'], args['ln_g'],
            args['ln_b'], args['w1'], args['b1'], args['w2'], args['b2'], inputs['L0_ffn_W2'].shape[1], out)
    r = _run(nc, [arrays], core_ids=[0])
    return r.results[0]["out_dram"]
```

```python
from contextlib import ExitStack

import concourse.bass as bass
from concourse import mybir

F32 = mybir.dt.float32
F32R = mybir.dt.float32r
BF16 = mybir.dt.bfloat16
ALU = mybir.AluOpType
ACT = mybir.ActivationFunctionType
AX_X = mybir.AxisListType.X

P = 128
HEADS = 16
DH = 64
HG = 4
GROUPS = HEADS // HG
SLOTS = 2 * GROUPS
QK_SCALE = 8.0
EPS = 1e-5
NORM_FLOOR_SQ = 1e-24
MASKED = -3.0e38
GATE_ROW = 64

C_IDENT, C_SHIFT, C_BAND, C_ROTA, C_ROTB, C_CAUSAL, C_CUMSUM, C_ROWS, C_PICK, C_END = (
    0, 128, 256, 384, 512, 640, 768, 896, 900, 1924)
MH = 8
MD = 32
M_EPS = 1e-6


def live(index, total):
    return not isinstance(index, int) or 0 <= index < total


def due(count):
    return not isinstance(count, int) or count > 0


def program(nc, x, ctxt, gate_w, gate_b, mln_scale, consts, wqkv, q_scale, k_scale, wo, ln_g, ln_b, w1, b1, w2, b2, F, out):
    NB, S, D = x.shape
    L = wqkv.shape[0]
    NPAIR = NB // 2
    NT = L * NPAIR
    TS = SLOTS * NT
    KC = D // P
    INNER = HEADS * DH
    GF = HG * DH
    QKV = 3 * GF
    UNITS = GROUPS * KC
    LEAD = (NB + 4) // 2
    SPLITS = L * UNITS
    LAST_SPLIT = SPLITS - LEAD
    OC = INNER // P
    FC = (F + P - 1) // P
    FREM = F - (FC - 1) * P
    fsize = [P] * (FC - 1) + [FREM]
    TOK = 2 * P

    with ExitStack() as ctx:
        def sb(name, shape, dt=F32):
            return ctx.enter_context(nc.sbuf_tensor(name, shape, dt))

        def ps(name):
            return ctx.enter_context(nc.psum_tensor(name, [P, 512], F32))

        def sem(name):
            return ctx.enter_context(nc.semaphore(name))

        pack = sb("pack", [P, C_END])
        ident = pack[:, C_IDENT:C_IDENT + P]
        shift = pack[:, C_SHIFT:C_SHIFT + P]
        rotA = pack[:, C_ROTA:C_ROTA + 2 * DH].rearrange("p (a d) -> p a d", a=2)
        rotB = pack[:, C_ROTB:C_ROTB + 2 * DH].rearrange("p (a d) -> p a d", a=2)
        ident_bf = sb("ident_bf", [P, P], BF16)
        band = pack[:, C_BAND:C_BAND + P].unsqueeze(1).unsqueeze(1).broadcast_to([P, 2, 2, P])
        neghalf = sb("neghalf", [P, 8])
        qk_gain = sb("qk_gain", [P, L, 2, DH])
        lng_col = sb("lng_col", [P, L, KC])
        lnb_col = sb("lnb_col", [P, L, KC])
        b1_col = sb("b1_col", [P, L, 2, FC])
        b2_row = sb("b2_row", [P, L, D])
        Wqkv = sb("Wqkv", [P, GROUPS * KC, 2, QKV], F32R)
        unit = sb("unit", [P, QKV])
        unit_split = sb("unit_split", [P, 2, QKV], F32R)
        split_dram = nc.dram_tensor("split_dram", [L, UNITS, P, 2, QKV], F32, kind="Internal").ap()
        Wo = sb("Wo", [P, OC, D])
        W1 = sb("W1", [P, 2 * FC - 1, KC, P])
        W2 = sb("W2", [P, FC, D])
        y = sb("y", [P, NB, D])
        x1 = sb("x1", [P, NB, D])

        arena = sb("arena", [P, 8, MH * P])

        def region(i, heads):
            return arena[:, i, :].rearrange("p (h t) -> p h t", h=heads)

        def half(i, j):
            return arena[:, i, j * 2 * GF:(j + 1) * 2 * GF]

        def half_by(i, j, heads):
            return half(i, j).rearrange("p (h t) -> p h t", h=heads)

        causal_bf = sb("causal_bf", [P, 4, P], BF16)
        row_scale = pack[:, C_ROWS:C_ROWS + 4]
        cumsum = pack[:, C_CUMSUM:C_CUMSUM + P]
        pick = pack[0:MH, C_PICK:C_PICK + MH * P].rearrange("k (h s) -> k h s", h=MH)
        Wg = sb("Wg", [P, 3 * KC, 2 * MH])
        gbias = sb("gbias", [P, 2 * MH])
        mscale = sb("mscale", [P, D])
        m_bst = sb("m_bst", [P, 6])
        m_mv = sb("m_mv", [P, 2])
        m_ve = sb("m_ve", [P, 1])
        m_rstd = sb("m_rstd", [P, 1])
        qln = [sb(f"qln{i}", [P, D]) for i in range(2)]
        cst = [sb(f"cst{i}", [P, D]) for i in range(2)]
        V33 = [sb(f"V33_{i}", [P, MH, MD + 1]) for i in range(2)]
        qcT = [half_by(7, i, 2 * KC) for i in range(2)]
        qm = [region(5 + i, MH) for i in range(2)]
        gts = [sb(f"gts{i}", [P, 2 * MH]) for i in range(2)]
        nf = sb("nf", [P, MH])
        ef = sb("ef", [P, MH])
        lf = sb("lf", [P, MH])
        logf = [sb(f"logf{i}", [P, MH]) for i in range(2)]
        csum = sb("csum", [P, MH])
        gg = sb("gg", [P, MH])
        gT = sb("gT", [MH, P])
        gmax = sb("gmax", [P, MH])
        mlog = sb("mlog", [P, MH])
        dm = region(0, MH)
        Dm = region(1, MH)
        en = [sb(f"en{i}", [P, MH]) for i in range(2)]
        Cm = [region(2 + i, MH) for i in range(2)]
        CT = region(4, MH)
        nrm = sb("nrm", [P, MH])
        nneg = sb("nneg", [P, MH])
        nrm2 = sb("nrm2", [P, MH])
        nrec = sb("nrec", [P, MH])
        hm = sb("hm", [P, D])
        h_bst = sb("h_bst", [P, 6])
        h_mv = sb("h_mv", [P, 2])
        h_ve = sb("h_ve", [P, 1])
        h_rstd = sb("h_rstd", [P, 1])
        hn = sb("hn", [P, D])
        hs = sb("hs", [P, D])
        f_bst = sb("f_bst", [P, 6])
        f_mv = sb("f_mv", [P, 2])
        f_ve = sb("f_ve", [P, 1])
        f_rstd = sb("f_rstd", [P, 1])

        ycur = [sb(f"ycur{i}", [P, D]) for i in range(2)]
        xT = [sb(f"xT{i}", [P, 2, KC, P], F32R) for i in range(2)]
        sq = half(0, 0)
        ss_raw = sb("ss_raw", [P, 8])
        ss = sb("ss", [P, 8])
        rq = sb("rq", [P, 8])
        tabA = sb("tabA", [P, 2, DH])
        tabB = sb("tabB", [P, 2, DH])
        qn = half(0, 1)
        u1 = half(1, 0)
        u2 = half(1, 1)
        u = [half(2, i) for i in range(2)]
        qkT = [half_by(3, i, 4) for i in range(2)]
        masked = half_by(6, 0, HG)
        mx = sb("mx", [P, HG])
        sc = [half_by(4, i, HG) for i in range(2)]
        pr = [half_by(5, i, HG) for i in range(2)]
        PTs = [sb(f"PTs{i}", [P, HG, P]) for i in range(2)]
        V65 = [sb(f"V65_{i}", [P, HG, DH + 1]) for i in range(4)]
        rec = sb("rec", [P, HG])
        O = [sb(f"O{i}", [P, GF]) for i in range(2)]
        OTs = region(7, OC)
        xs = sb("xs", [P, 2, P])
        bst = sb("bst", [P, 2, 2, 6])
        mv = sb("mv", [P, 2, 2])
        ve = sb("ve", [P, 2])
        rstd = sb("rstd", [P, 2])
        wait_carrier = sb("wait_carrier", [P, 1])
        xn = sb("xn", [P, 2, D])
        zT = sb("zT", [P, KC, TOK])
        gel = [sb(f"gel{i}", [P, TOK]) for i in range(2)]
        hT = sb("hT", [P, FC, TOK])
        ffo = sb("ffo", [P, D])

        bQK, bV, bPVO, bPT, bTR, bY = [ps(n) for n in ("bQK", "bV", "bPVO", "bPT", "bTR", "bY")]
        bSIM = ctx.enter_context(nc.psum_tensor("bSIM", [P, 2, 512], F32))
        sims = bSIM[:, :, 0:2 * P].rearrange("p r (i j) -> p r i j", i=2)

        first_in = sem("first_in")
        rest_in = sem("rest_in")
        const_in = sem("const_in")
        pool_const = sem("pool_const")
        dve_const = sem("dve_const")
        wqkv_in = [sem(f"wqkv_in{g}") for g in range(GROUPS)]
        wo_in = sem("wo_in")
        unit_in, hi_ready, lo_ready, split_out = [sem(n) for n in ("unit_in", "hi_ready", "lo_ready", "split_out")]
        xlo_ready = sem("xlo_ready")
        w1_in = [sem(f"w1_in{c}") for c in range(FC)]
        w2_in = sem("w2_in")
        out_done = sem("out_done")
        qk_done, v_done, sim_done, pv_done, ot_done, pt_done, tr_done = [
            sem(n) for n in ("qk_done", "v_done", "sim_done", "pv_done", "ot_done", "pt_done", "tr_done")]
        wo_done, w1_done, w2_done, xt_done, sh_done, zt_done = [
            sem(n) for n in ("wo_done", "w1_done", "w2_done", "xt_done", "sh_done", "zt_done")]
        sq_ready, v_ready, exp_ready, ots_ready, pts_ready, qkt_ready = [
            sem(n) for n in ("sq_ready", "v_ready", "exp_ready", "ots_ready", "pts_ready", "qkt_ready")]
        gelu_ready, xts_ready, sh_ready, z_ready = [sem(n) for n in ("gelu_ready", "xts_ready", "sh_ready", "z_ready")]
        ssr_ready, ss_ready, qn_ready, u1_ready, mx_ready, sub_ready, rec_ready, on_ready = [
            sem(n) for n in ("ssr_ready", "ss_ready", "qn_ready", "u1_ready", "mx_ready", "sub_ready", "rec_ready", "on_ready")]
        h_ready, y1_ready, y_ready, ffo_ready, bst_ready, mv_ready, ve_ready, xn_ready = [
            sem(n) for n in ("h_ready", "y1_ready", "y_ready", "ffo_ready", "bst_ready", "mv_ready", "ve_ready", "xn_ready")]
        rq_ready, u2_ready, u_ready, tab_ready, ycur_ready, rstd_ready = [
            sem(n) for n in ("rq_ready", "u2_ready", "u_ready", "tab_ready", "ycur_ready", "rstd_ready")]

        mq_bst, mq_mv, mq_ve, mq_rstd, mq_ready, mc_ready, mT_done, mT_ready, qm_ready = [
            sem(n) for n in ("mq_bst", "mq_mv", "mq_ve", "mq_rstd", "mq_ready", "mc_ready", "mT_done", "mT_ready", "qm_ready")]
        mg_done, gts_ready, nf_ready, ef_ready, lf_ready, logf_ready = [
            sem(n) for n in ("mg_done", "gts_ready", "nf_ready", "ef_ready", "lf_ready", "logf_ready")]
        cs_done, cs_ready, gg_ready, gT_done, gT_ready, mqk_done, gb_done, gmax_ready, dm_ready, mlog_ready = [
            sem(n) for n in ("cs_done", "cs_ready", "gg_ready", "gT_done", "gT_ready", "mqk_done", "gb_done", "gmax_ready",
                             "dm_ready", "mlog_ready")]
        Dm_ready, en_ready, Cm_ready, CT_done, CT_ready, v33_ready, mpv_done = [
            sem(n) for n in ("Dm_ready", "en_ready", "Cm_ready", "CT_done", "CT_ready", "v33_ready", "mpv_done")]
        nrm_ready, nrm2_ready, nrec_ready, hm_ready, mh_bst, mh_mv, mh_ve, mh_rstd, hn_ready, hs_ready = [
            sem(n) for n in ("nrm_ready", "nrm2_ready", "nrec_ready", "hm_ready", "mh_bst", "mh_mv", "mh_ve", "mh_rstd",
                             "hn_ready", "hs_ready")]
        masked_ready = sem("masked_ready")
        nneg_ready = sem("nneg_ready")
        x1_ready, mf_bst, mf_mv, mf_ve, mf_rstd, res_ready = [
            sem(n) for n in ("x1_ready", "mf_bst", "mf_mv", "mf_ve", "mf_rstd", "res_ready")]

        block = ctx.enter_context(nc.Block())

        def m_sweep(eng, step):
            for b in range(4):
                step(b, b % 2)
            with eng.Fori(4, NB - 3, 2) as b:
                step(b, 0)
                step(b + 1, 1)
            for b in range(NB - 2, NB + 3):
                step(b, b % 2)

        def sweep(eng, body):
            body(0)
            body(1)
            with eng.Fori(0, (L - 3) * NPAIR + 1, NPAIR) as base:
                with eng.Fori(2, NPAIR - 1) as pair:
                    body(base + pair)
                body(base + NPAIR - 1, refill=True)
                body(base + NPAIR)
                body(base + NPAIR + 1)
            with eng.Fori((L - 2) * NPAIR + 2, LAST_SPLIT) as n:
                body(n)
            for n in range(LAST_SPLIT, (L - 1) * NPAIR):
                body(n, split=False, refill=n == (L - 1) * NPAIR - 1)
            with eng.Fori((L - 1) * NPAIR, NT) as n:
                body(n, split=False)
            body(NT)
            body(NT + 1)

        @block.sync
        def _(sp):
            sp.dma_start(x1[:, 0:2], x[0:2].rearrange("b s d -> s b d")).then_inc(first_in, 16)
            sp.dma_start(y[:, 0:2], ctxt[0:2].rearrange("b s d -> s b d")).then_inc(first_in, 16)
            sp.dma_start(pack[:], consts).then_inc(first_in, 16)
            sp.dma_start(Wg[:], gate_w).then_inc(first_in, 16)
            sp.dma_start(gbias[:], gate_b.broadcast_to([P, 2 * MH])).then_inc(first_in, 16)
            sp.dma_start(mscale[:], mln_scale.broadcast_to([P, D])).then_inc(first_in, 16)
            sp.dma_start(x1[:, 2:NB], x[2:NB].rearrange("b s d -> s b d")).then_inc(rest_in, 16)
            sp.dma_start(y[:, 2:NB], ctxt[2:NB].rearrange("b s d -> s b d")).then_inc(rest_in, 16)
            ld = lambda d, s: sp.dma_start(d, s).then_inc(const_in, 16)
            for l in range(L):
                ld(qk_gain[:, l, 0, :], q_scale[l:l + 1, :].broadcast_to([P, DH]))
                ld(qk_gain[:, l, 1, :], k_scale[l:l + 1, :].broadcast_to([P, DH]))
                ld(b2_row[:, l, :], b2[l:l + 1, :].broadcast_to([P, D]))
            ld(lng_col[:], ln_g)
            ld(lnb_col[:], ln_b)
            ld(b1_col[:], b1)

            def load_layer(l):
                if due(NB * l):
                    sp.wait_ge(wo_done, NB * l)
                sp.dma_start(Wo[:], wo[l]).then_inc(wo_in, 16)
                for c in range(FC):
                    if due(FC * NPAIR * l - FC + c + 1):
                        sp.wait_ge(w1_done, FC * NPAIR * l - FC + c + 1)
                    sp.dma_start(W1[:, 2 * c:min(2 * c + 2, 2 * FC - 1)], w1[l, :, 2 * c:min(2 * c + 2, 2 * FC - 1)]).then_inc(w1_in[c], 16)
                if due(NB * l):
                    sp.wait_ge(w2_done, NB * l)
                sp.dma_start(W2[:], w2[l]).then_inc(w2_in, 16)

            load_layer(0)
            with sp.Fori(1, L) as l:
                load_layer(l)
            for i in range(4):
                sp.wait_ge(res_ready, i + 1)
                q = slice(i * NB // 4, (i + 1) * NB // 4)
                sp.dma_start(out[q].rearrange("b s d -> s b d"), y[:, q, :]).then_inc(out_done, 16)
            sp.wait_ge(out_done, 64)
            sp.wait_ge(split_out, 16 * SPLITS)

        n_first = 6
        n_const = 3 * L + 3

        @block.tensor
        def _(pe):
            mm = nc.tensor.matmul
            terms = [(a, w, c) for a, w in ((1, 0), (0, 1), (0, 0)) for c in range(KC)]

            def transpose_y(G, par, s):
                pe.wait_ge(ycur_ready, G + 1)
                if live(s - 3, TS):
                    pe.wait_ge(pts_ready, s - 2)
                for c in range(KC):
                    last = nc.tensor.transpose(bPT[:, c * P:(c + 1) * P], ycur[par][:, c * P:(c + 1) * P], ident)
                last.then_inc(xt_done, 1)

            def body(n, split=True, refill=False):
                layer = n // NPAIR
                for k in range(SLOTS):
                    s = SLOTS * n + k
                    g, second = k % GROUPS, k // GROUPS
                    if live(s, TS):
                        pe.wait_ge(xts_ready, 2 * n + second + 1)
                        pe.wait_ge(xlo_ready, 2 * n + second + 1)
                        pe.wait_ge(wqkv_in[g], 16 * (layer + 1))
                        if due(s):
                            pe.wait_ge(qn_ready, s)
                        for t, (a, w, c) in enumerate(terms):
                            last = mm(bQK[:], xT[second][:, a, c, :], Wqkv[:, g * KC + c, w, 0:2 * GF], start=t == 0, stop=t == len(terms) - 1)
                        last.then_inc(qk_done, 1)
                    i = s - 3
                    if live(i, TS):
                        pe.wait_ge(exp_ready, i + 1)
                        if due(i):
                            pe.wait_ge(pts_ready, i)
                        if k in (0, 4):
                            G = 2 * n + (1 if k == 4 else 0)
                            if live(G, 2 * NT + 1):
                                pe.wait_ge(xlo_ready, G + 1)
                        elif k == 5:
                            if due(n):
                                pe.wait_ge(sh_ready, n)
                        elif k == 6:
                            if due(n):
                                pe.wait_ge(z_ready, n)
                        for h in range(HG):
                            last = nc.tensor.transpose(bPT[:, h * P:(h + 1) * P], pr[(k + 1) % 2][:, h, :], ident)
                        last.then_inc(pt_done, 1)
                    i = s - 2
                    if live(i, TS):
                        pe.wait_ge(qkt_ready, i + 1)
                        if due(i):
                            pe.wait_ge(masked_ready, i)
                        for h in range(HG):
                            r0 = DH * (h % 2)
                            last = mm(bSIM[:, h % 2, (h // 2) * P:(h // 2 + 1) * P], qkT[k % 2][r0:r0 + DH, h // 2, :],
                                      qkT[k % 2][r0:r0 + DH, 2 + h // 2, :], start=True, stop=True)
                        last.then_inc(sim_done, 1)
                    if live(s, TS):
                        if due(s):
                            pe.wait_ge(v_ready, s)
                        if k == 0:
                            if due(2 * n - 1):
                                pe.wait_ge(y1_ready, 2 * n - 1)
                        if k == 4:
                            if due(2 * n):
                                pe.wait_ge(y1_ready, 2 * n)
                        if k == 5:
                            if due(2 * n - 3):
                                pe.wait_ge(ffo_ready, 2 * n - 3)
                        if k == 6:
                            if due(2 * n - 2):
                                pe.wait_ge(ffo_ready, 2 * n - 2)
                        for t, (a, w, c) in enumerate(terms):
                            last = mm(bV[:, 0:GF], xT[second][:, a, c, :], Wqkv[:, g * KC + c, w, 2 * GF:QKV], start=t == 0, stop=t == len(terms) - 1)
                        last.then_inc(v_done, 1)
                    i = s - 3
                    if live(i, TS):
                        pe.wait_ge(pts_ready, i + 1)
                        pe.wait_ge(v_ready, i + 1)
                        if due(i):
                            pe.wait_ge(ots_ready, i)
                        for h in range(HG):
                            last = mm(bPVO[:, h * 65:h * 65 + 65], PTs[(k + 1) % 2][:, (h % 2) * 2 + h // 2, :], V65[(k + 1) % 4][:, h, :],
                                      start=True, stop=True)
                        last.then_inc(pv_done, 1)
                    if k in (3, 7):
                        G = 2 * n + (1 if k == 3 else 2)
                        if live(G, 2 * NT + 1):
                            transpose_y(G, 1 if k == 3 else 0, s)
                    if k == 4 and live(n - 1, NT):
                        if due(2 * n):
                            pe.wait_ge(y1_ready, 2 * n)
                        if live(s - 3, TS):
                            pe.wait_ge(pts_ready, s - 2)
                        for b in range(2):
                            bi = (2 * (n - 1) + b) % NB
                            last = mm(bPT[:, b * P:(b + 1) * P], shift, y[:, bi, P:D], start=True, stop=True)
                        last.then_inc(sh_done, 1)
                    if k == 5 and live(n - 1, NT):
                        if due(n):
                            pe.wait_ge(xn_ready, n)
                        if live(s - 3, TS):
                            pe.wait_ge(pts_ready, s - 2)
                        for c in range(KC):
                            for b in range(2):
                                last = nc.tensor.transpose(bPT[:, (2 * c + b) * P:(2 * c + b + 1) * P],
                                                           xn[:, b, c * P:(c + 1) * P], ident)
                        last.then_inc(zt_done, 1)
                    G = 2 * n - 1 if k == 3 else 2 * n
                    if k in (3, 7) and live(G, 2 * NT):
                        pe.wait_ge(ots_ready, 4 * G + 4)
                        pe.wait_ge(wo_in, 16 * (G // NB + 1))
                        if due(s + 1 if live(s, TS) else 0):
                            pe.wait_ge(v_ready, s + 1 if live(s, TS) else 0)
                        for c in range(OC):
                            last = mm(bV[:, 0:D], OTs[:, c, :], Wo[:, c, :], start=c == 0, stop=c == OC - 1)
                        last.then_inc(wo_done, 1)
                    G = 2 * (n - 2) + (k - 4)
                    if k in (4, 5) and live(G, 2 * NT):
                        if due(FC * (n - 1)):
                            pe.wait_ge(h_ready, FC * (n - 1))
                        pe.wait_ge(w2_in, 16 * (G // NB + 1))
                        if live(s, TS):
                            pe.wait_ge(v_ready, s + 1)
                        elif k == 4:
                            if due(min(2 * n, 2 * NT)):
                                pe.wait_ge(y1_ready, min(2 * n, 2 * NT))
                        else:
                            if due(NB + G):
                                pe.wait_ge(y_ready, NB + G)
                        for c in range(FC):
                            last = mm(bV[:, 0:D], hT[0:fsize[c], c, (k - 4) * P:(k - 3) * P], W2[0:fsize[c], c, :],
                                      start=c == 0, stop=c == FC - 1)
                        last.then_inc(w2_done, 1)
                    m, c1 = (n - 1, k - 6) if k >= 6 else (n - 2, k + 2)
                    if k not in (4, 5) and live(m, NT):
                        idx = FC * m + c1
                        if c1 == 0:
                            pe.wait_ge(z_ready, m + 1)
                        pe.wait_ge(w1_in[c1], 16 * (m // NPAIR + 1))
                        if due(idx):
                            pe.wait_ge(h_ready, idx)
                        for a in range(2 if c1 < FC - 1 else 1):
                            for c in range(KC):
                                last = mm(bY[:, a * TOK:(a + 1) * TOK], W1[:, 2 * c1 + a, c, :], zT[:, c, :],
                                          start=c == 0, stop=c == KC - 1)
                        last.then_inc(w1_done, 1)
                    i = s - 3
                    if live(i, TS):
                        pe.wait_ge(on_ready, i + 1)
                        for j in range(2):
                            last = nc.tensor.transpose(bPVO[:, j * P:(j + 1) * P], O[(k + 1) % 2][:, j * P:(j + 1) * P], ident)
                        last.then_inc(ot_done, 1)
                    i = s - 1
                    if live(i, TS):
                        pe.wait_ge(u_ready, i + 1)
                        if due(i):
                            pe.wait_ge(qkt_ready, i)
                        for j in range(4):
                            last = nc.tensor.transpose(bTR[:, j * P:(j + 1) * P], u[(k + 1) % 2][:, j * P:(j + 1) * P], ident)
                        last.then_inc(tr_done, 1)

            def transpose_inputs(b, par):
                pe.wait_ge(mq_ready, b + 1)
                pe.wait_ge(mc_ready, b + 1)
                if due(b):
                    pe.wait_ge(mT_ready, b)
                for a, src in enumerate((qln[par], cst[par])):
                    for c in range(KC):
                        last = nc.tensor.transpose(bQK[:, (a * KC + c) * P:(a * KC + c + 1) * P], src[:, c * P:(c + 1) * P], ident)
                last.then_inc(mT_done, 1)

            def gates(b, par):
                pe.wait_ge(mT_ready, b + 1)
                if due(b):
                    pe.wait_ge(cs_ready, b)
                for c in range(3 * KC):
                    src = qcT[par][:, c if c < 2 * KC else c - KC, :]
                    last = mm(bY[:, 2 * MH:4 * MH], src, Wg[:, c, :], start=c == 0, stop=c == 3 * KC - 1)
                last.then_inc(mg_done, 1)

            def m_step(b, par):
                i, j = b - 1, b - 2
                if live(i, NB):
                    pe.wait_ge(gT_ready, i + 1)
                    if due(i):
                        pe.wait_ge(dm_ready, i)
                    for r in range(2):
                        mm(bSIM[:, r, :], ident_bf[:], causal_bf[:].rearrange("p h t -> p (h t)"), start=True, stop=False,
                           skip_group_check=True)
                        for h in range(4):
                            last = mm(bSIM[:, r, h * P:(h + 1) * P], pick[:, 4 * r + h, :], gT[:], start=False, stop=h == 3,
                                      skip_group_check=True)
                    last.then_inc(gb_done, 1)
                if live(b, NB):
                    pe.wait_ge(logf_ready, b + 1)
                    mm(bY[:, 0:MH], cumsum, logf[par][:], start=True, stop=True).then_inc(cs_done, 1)
                if live(i, NB):
                    if due(i):
                        pe.wait_ge(CT_ready, i)
                    pe.wait_ge(qm_ready, i + 1)
                    for h in range(MH):
                        bank = bPT if h < 4 else bTR
                        last = mm(bank[:, (h % 4) * P:(h % 4 + 1) * P], qm[1 - par][:, h, :], qcT[1 - par][:, KC + h // 4, :],
                                  start=True, stop=True)
                    last.then_inc(mqk_done, 1)
                if live(b + 1, NB):
                    transpose_inputs(b + 1, 1 - par)
                if live(j, NB):
                    pe.wait_ge(CT_ready, j + 1)
                    pe.wait_ge(v33_ready, j + 1)
                    if due(j):
                        pe.wait_ge(hm_ready, j)
                    for h in range(MH):
                        last = mm(bV[:, h * (MD + 1):(h + 1) * (MD + 1)], CT[:, h, :], V33[par][:, h, :], start=True, stop=True)
                    last.then_inc(mpv_done, 1)
                if live(b + 1, NB):
                    gates(b + 1, 1 - par)
                if live(b, NB):
                    pe.wait_ge(gg_ready, b + 1)
                    if due(b):
                        pe.wait_ge(gT_ready, b)
                    nc.tensor.transpose(bPVO[0:MH, 0:P], gg[:], ident).then_inc(gT_done, 1)
                if live(i, NB):
                    pe.wait_ge(Cm_ready, i + 1)
                    for h in range(MH):
                        bank = bPT if h < 4 else bTR
                        last = nc.tensor.transpose(bank[:, (h % 4) * P:(h % 4 + 1) * P], Cm[1 - par][:, h, :], ident)
                    last.then_inc(CT_done, 1)

            pe.wait_ge(first_in, 16 * n_first)
            pe.wait_ge(dve_const, 3)
            transpose_inputs(0, 0)
            gates(0, 0)
            m_sweep(pe, m_step)
            pe.wait_ge(const_in, 16 * n_const)
            pe.wait_ge(y_ready, NB)
            transpose_y(0, 0, 0)
            sweep(pe, body)

        @block.scalar
        def _(act):
            fn = nc.scalar.activation

            def evacuate_xT(G, par):
                act.wait_ge(xt_done, G + 1)
                if due(4 * (G - 1)):
                    act.wait_ge(v_done, 4 * (G - 1))
                fn(xT[par][:, 0, 0, :], bPT[:, 0:P], ACT.Copy)
                fn(xT[par][:, 0, 1, 1:P], bPT[:, P:2 * P - 1], ACT.Copy).then_inc(xts_ready, 1)

            def load_unit(w):
                if due(w):
                    act.wait_ge(lo_ready, w)
                act.dma_start(unit[:], wqkv[w // UNITS, w % UNITS]).then_inc(unit_in, 16)

            def split_unit(w):
                act.wait_ge(unit_in, 16 * (w + 1))
                if due(w):
                    act.wait_ge(split_out, 16 * w)
                fn(unit_split[:, 0, :], unit[:], ACT.Copy).then_inc(hi_ready, 1)

            def store_unit(w):
                act.wait_ge(lo_ready, w + 1)
                act.dma_start(split_dram[w // UNITS, w % UNITS], unit_split[:].bitcast(F32)).then_inc(split_out, 16)

            def body(n, split=True, refill=False):
                for k in range(SLOTS):
                    s = SLOTS * n + k
                    if split and live(n + LEAD, SPLITS):
                        if k == 0:
                            load_unit(n + LEAD)
                        elif k == 4:
                            split_unit(n + LEAD)
                        elif k == 7:
                            store_unit(n + LEAD)
                    if live(s, TS):
                        act.wait_ge(qk_done, s + 1)
                        if due(s):
                            act.wait_ge(ssr_ready, s)
                        fn(sq[:], bQK[:], ACT.Square).then_inc(sq_ready, 1)
                    i = s - 4
                    if live(i, TS):
                        act.wait_ge(ot_done, i + 1)
                        if k == 4:
                            if due(2 * n):
                                act.wait_ge(wo_done, 2 * n)
                        if k == 0:
                            if due(2 * n - 1):
                                act.wait_ge(wo_done, 2 * n - 1)
                        g = k % 4
                        fn(OTs[:, 2 * g:2 * g + 2, :].rearrange("p c t -> p (c t)"), bPVO[:, 0:GF], ACT.Copy).then_inc(ots_ready, 1)
                    i = s - 3
                    if live(i, TS):
                        act.wait_ge(pt_done, i + 1)
                        if due(i - 1):
                            act.wait_ge(pv_done, i - 1)
                        fn(PTs[(k + 1) % 2][:].rearrange("p h t -> p (h t)"), bPT[:], ACT.Copy).then_inc(pts_ready, 1)
                    if live(s, TS):
                        act.wait_ge(v_done, s + 1)
                        if due(s - 3):
                            act.wait_ge(pv_done, s - 3)
                        fn(V65[k % 4][:, :, 0:DH], bV[:, 0:GF].rearrange("p (h d) -> p h d", h=HG), ACT.Copy).then_inc(v_ready, 1)
                    if k in (3, 7):
                        G = 2 * n + (1 if k == 3 else 2)
                        if live(G, 2 * NT + 1):
                            evacuate_xT(G, 1 if k == 3 else 0)
                    if k == 4 and live(n - 1, NT):
                        if due(n):
                            act.wait_ge(sh_done, n)
                        if due(n - 1):
                            act.wait_ge(xn_ready, n - 1)
                        fn(xs[:].rearrange("p b d -> p (b d)"), bPT[:, 0:TOK], ACT.Copy).then_inc(sh_ready, 1)
                    if k == 5 and live(n - 1, NT):
                        lm = (n - 1) // NPAIR
                        if due(n):
                            act.wait_ge(zt_done, n)
                        if due(FC * (n - 1)):
                            act.wait_ge(w1_done, FC * (n - 1))
                        for c in range(KC):
                            last = fn(zT[:, c, :], bPT[:, c * TOK:(c + 1) * TOK], ACT.Identity,
                                      bias=lnb_col[:, lm, c:c + 1], scale=lng_col[:, lm, c:c + 1])
                        last.then_inc(z_ready, 1)
                    i = s - 2
                    if live(i, TS):
                        act.wait_ge(sub_ready, i + 1)
                        if due(i - 1):
                            act.wait_ge(pt_done, i - 1)
                        fn(pr[k % 2][:], sc[k % 2][:], ACT.Exp).then_inc(exp_ready, 1)
                    m, c1 = (n - 1, k - 6) if k >= 6 else (n - 2, k + 2)
                    if k not in (4, 5) and live(m, NT):
                        idx = FC * m + c1
                        lm = m // NPAIR
                        f = fsize[c1]
                        act.wait_ge(w1_done, idx + 1)
                        if due(idx - 1):
                            act.wait_ge(h_ready, idx - 1)
                        p0, t0 = (0, TOK) if c1 < FC - 1 else (GATE_ROW, 0)
                        fn(gel[c1 % 2][0:f, :], bY[p0:p0 + f, t0:t0 + TOK], ACT.Gelu, bias=b1_col[p0:p0 + f, lm, 1, c1:c1 + 1]).then_inc(gelu_ready, 1)

            def evacuate_inputs(b, par):
                act.wait_ge(mT_done, b + 1)
                if due(b - 1):
                    act.wait_ge(mqk_done, b - 1)
                fn(qcT[par][:].rearrange("p c t -> p (c t)"), bQK[:], ACT.Copy).then_inc(mT_ready, 1)

            def log_gates(b):
                act.wait_ge(nf_ready, b + 1)
                if due(b):
                    act.wait_ge(lf_ready, b)
                fn(ef[:], nf[:], ACT.Exp).then_inc(ef_ready, 1)
                act.wait_ge(ef_ready, b + 1)
                if due(b):
                    act.wait_ge(logf_ready, b)
                fn(lf[:], ef[:], ACT.Ln, bias=1.0).then_inc(lf_ready, 1)

            def m_step(b, par):
                i = b - 1
                if par == 0:
                    if due(b):
                        store_unit(b // 2 - 1)
                    load_unit(b // 2)
                if live(i, NB):
                    act.wait_ge(dm_ready, i + 1)
                    if due(i):
                        act.wait_ge(Cm_ready, i)
                    fn(Dm[:], dm[:], ACT.Exp).then_inc(Dm_ready, 1)
                    act.wait_ge(mlog_ready, i + 1)
                    if due(i - 1):
                        act.wait_ge(nneg_ready, i - 1)
                    fn(en[1 - par][:], mlog[:], ACT.Exp, scale=-1.0).then_inc(en_ready, 1)
                if live(b + 1, NB):
                    evacuate_inputs(b + 1, 1 - par)
                if live(b, NB):
                    act.wait_ge(gT_done, b + 1)
                    if due(b):
                        act.wait_ge(gb_done, b)
                    fn(gT[:], bPVO[0:MH, 0:P], ACT.Copy).then_inc(gT_ready, 1)
                    act.wait_ge(mc_ready, b + 1)
                    if due(b - 1):
                        act.wait_ge(mpv_done, b - 1)
                    fn(V33[par][:, :, 0:MD], cst[par][:].rearrange("p (h d) -> p h d", h=MH), ACT.Copy).then_inc(v33_ready, 1)
                if live(i, NB):
                    act.wait_ge(CT_done, i + 1)
                    if due(i):
                        act.wait_ge(mpv_done, i)
                    fn(CT[:, 0:4].rearrange("p h t -> p (h t)"), bPT[:], ACT.Copy)
                    fn(CT[:, 4:8].rearrange("p h t -> p (h t)"), bTR[:], ACT.Copy).then_inc(CT_ready, 1)
                if live(b + 1, NB):
                    log_gates(b + 1)
                if par == 0:
                    split_unit(b // 2)

            act.wait_ge(dve_const, 3)
            evacuate_inputs(0, 0)
            log_gates(0)
            m_sweep(act, m_step)
            store_unit(LEAD - 1)
            act.wait_ge(const_in, 16 * n_const)
            evacuate_xT(0, 0)
            sweep(act, body)

        @block.vector
        def _(dve):
            V = nc.vector

            def residual(G):
                dve.wait_ge(wo_done, G + 1)
                dve.wait_ge(y_ready, G + 1)
                b = G % NB
                V.tensor_tensor(y[:, b, :], y[:, b, :], bV[:, 0:D], ALU.add).then_inc(y1_ready, 1)

            def final_add(G):
                b, lm = G % NB, G // NB
                dve.wait_ge(w2_done, G + 1)
                V.tensor_tensor(ffo[:], bV[:, 0:D], b2_row[:, lm, :], ALU.add).then_inc(ffo_ready, 1)
                dve.wait_ge(ffo_ready, G + 1)
                V.tensor_tensor(y[:, b, :], y[:, b, :], ffo[:], ALU.add).then_inc(y_ready, 1)

            def lower_xT(G, par):
                dve.wait_ge(xts_ready, G + 1)
                V.tensor_tensor(xT[par][:, 1, 0, :], bPT[:, 0:P], xT[par][:, 0, 0, :], ALU.subtract)
                V.tensor_tensor(xT[par][:, 1, 1, 1:P], bPT[:, P:2 * P - 1], xT[par][:, 0, 1, 1:P], ALU.subtract).then_inc(xlo_ready, 1)

            def body(n, split=True, refill=False):
                for k in range(SLOTS):
                    s = SLOTS * n + k
                    if live(s, TS):
                        dve.wait_ge(sq_ready, s + 1)
                        if due(s):
                            dve.wait_ge(ss_ready, s)
                        V.tensor_reduce(ss_raw[:], sq[:].rearrange("p (h d) -> p h d", d=DH), axis=AX_X, op=ALU.add).then_inc(ssr_ready, 1)
                        dve.wait_ge(ssr_ready, s + 1)
                        if due(s):
                            dve.wait_ge(rq_ready, s)
                        V.tensor_scalar_max(ss[:], ss_raw[:], NORM_FLOOR_SQ).then_inc(ss_ready, 1)
                    if k == 5 and live(n - 1, NT):
                        if due(n):
                            dve.wait_ge(rstd_ready, n)
                        if due(n - 1):
                            dve.wait_ge(zt_done, n - 1)
                        for b in range(2):
                            bi = (2 * (n - 1) + b) % NB
                            V.tensor_scalar(xn[:, b, 0:P], y[:, bi, 0:P], mv[:, b, 0:1], rstd[:, b:b + 1], ALU.subtract, ALU.mult)
                            last = V.tensor_scalar(xn[:, b, P:D], xs[:, b, :], mv[:, b, 0:1], rstd[:, b:b + 1], ALU.subtract, ALU.mult)
                        last.then_inc(xn_ready, 1)
                    i = s - 2
                    if live(i, TS):
                        dve.wait_ge(sim_done, i + 1)
                        if due(i):
                            dve.wait_ge(sub_ready, i)
                        V.tensor_tensor(masked[:].rearrange("p (r i) j -> p r i j", r=2), sims, band, ALU.add).then_inc(masked_ready, 1)
                        dve.wait_ge(masked_ready, i + 1)
                        V.tensor_reduce(mx[:], masked[:], axis=AX_X, op=ALU.max).then_inc(mx_ready, 1)
                    i = s - 3
                    if live(i, TS):
                        pv = bPVO[:, 0:HG * 65].rearrange("p (h d) -> p h d", h=HG)
                        dve.wait_ge(pv_done, i + 1)
                        if due(i):
                            dve.wait_ge(on_ready, i)
                        V.reciprocal(rec[:].unsqueeze(2), pv[:, :, DH:DH + 1]).then_inc(rec_ready, 1)
                        dve.wait_ge(rec_ready, i + 1)
                        if due(i - 1):
                            dve.wait_ge(ot_done, i - 1)
                        V.tensor_tensor(O[(k + 1) % 2][:].rearrange("p (h d) -> p h d", h=HG), pv[:, :, 0:DH],
                                        rec[:].unsqueeze(2).broadcast_to([P, HG, DH]), ALU.mult).then_inc(on_ready, 1)
                    i = s - 2
                    if live(i, TS):
                        dve.wait_ge(mx_ready, i + 1)
                        if due(i - 1):
                            dve.wait_ge(exp_ready, i - 1)
                        V.tensor_tensor(sc[k % 2][:], masked[:], mx[:].unsqueeze(2).broadcast_to([P, HG, P]),
                                        ALU.subtract).then_inc(sub_ready, 1)
                    if live(s, TS):
                        dve.wait_ge(rq_ready, s + 1)
                        if due(s):
                            dve.wait_ge(u_ready, s)
                        V.tensor_tensor(qn[:].rearrange("p (h d) -> p h d", d=DH), bQK[:].rearrange("p (h d) -> p h d", d=DH),
                                        rq[:].unsqueeze(2).broadcast_to([P, 2 * HG, DH]), ALU.mult).then_inc(qn_ready, 1)
                        dve.wait_ge(qn_ready, s + 1)
                        dve.wait_ge(tab_ready, n + 1)
                        V.tensor_tensor(u1[:].rearrange("p (a h d) -> p a h d", a=2, h=HG), qn[:].rearrange("p (a h d) -> p a h d", a=2, h=HG),
                                        tabA[:].unsqueeze(2).broadcast_to([P, 2, HG, DH]), ALU.mult).then_inc(u1_ready, 1)
                    if k in (3, 7):
                        G = 2 * n + (1 if k == 3 else 2)
                        if live(G, 2 * NT + 1):
                            lower_xT(G, 1 if k == 3 else 0)
                    if k == 3 and live(2 * n - 1, 2 * NT):
                        residual(2 * n - 1)
                    if k == 7 and live(2 * n, 2 * NT):
                        residual(2 * n)
                    if k == 4 and live(n - 1, NT):
                        if due(n):
                            dve.wait_ge(sh_ready, n)
                        if due(2 * n):
                            dve.wait_ge(y1_ready, 2 * n)
                        if due(n - 1):
                            dve.wait_ge(mv_ready, n - 1)
                        V.memset(wait_carrier[:], 0.0)
                        for b in range(2):
                            bi = (2 * (n - 1) + b) % NB
                            V.bn_stats(bst[:, b, 0, :], y[:, bi, 0:P])
                            last = V.bn_stats(bst[:, b, 1, :], xs[:, b, :])
                        last.then_inc(bst_ready, 1)
                        if due(n):
                            dve.wait_ge(bst_ready, n)
                        if due(n - 1):
                            dve.wait_ge(xn_ready, n - 1)
                        V.memset(wait_carrier[:], 0.0)
                        V.bn_aggr(mv[:, 0, :], bst[:, 0].rearrange("p a b -> p (a b)"))
                        V.bn_aggr(mv[:, 1, :], bst[:, 1].rearrange("p a b -> p (a b)")).then_inc(mv_ready, 1)
                        if due(n):
                            dve.wait_ge(mv_ready, n)
                        if due(n - 1):
                            dve.wait_ge(rstd_ready, n - 1)
                        V.tensor_scalar_add(ve[:], mv[:, :, 1], EPS).then_inc(ve_ready, 1)
                    G = 2 * (n - 2) + (k - 4)
                    if k in (4, 5) and live(G, 2 * NT):
                        final_add(G)
                    i = s - 1
                    if live(i, TS):
                        dve.wait_ge(tr_done, i + 1)
                        if due(i - 1):
                            dve.wait_ge(sim_done, i - 1)
                        V.tensor_copy(qkT[(k + 1) % 2][:].rearrange("p c t -> p (c t)"), bTR[:]).then_inc(qkt_ready, 1)
                    m, c1 = (n - 1, k - 6) if k >= 6 else (n - 2, k + 2)
                    if k not in (4, 5) and live(m, NT):
                        idx = FC * m + c1
                        lm = m // NPAIR
                        f = fsize[c1]
                        dve.wait_ge(gelu_ready, idx + 1)
                        if c1 == 0:
                            if due(2 * m):
                                dve.wait_ge(w2_done, 2 * m)
                        V.scalar_tensor_tensor(hT[0:f, c1, :], bY[0:f, 0:TOK], b1_col[0:f, lm, 0, c1:c1 + 1], gel[c1 % 2][0:f, :],
                                               op0=ALU.add, op1=ALU.mult).then_inc(h_ready, 1)
                    if split and k == 5 and live(n + LEAD, SPLITS):
                        w = n + LEAD
                        dve.wait_ge(hi_ready, w + 1)
                        if due(w):
                            dve.wait_ge(split_out, 16 * w)
                        V.tensor_tensor(unit_split[:, 1, :], unit[:], unit_split[:, 0, :], ALU.subtract).then_inc(lo_ready, 1)

            dve.wait_ge(first_in, 16 * n_first)
            V.tensor_copy(ident_bf[:], ident).then_inc(dve_const, 1)
            for i in range(2):
                V.memset(xT[i][:, :, 1, 0:1].bitcast(F32), 0.0)
            for i in range(4):
                last = V.memset(V65[i][:, :, DH:DH + 1], 1.0)
            last.then_inc(dve_const, 1)
            V.tensor_copy(causal_bf[:], pack[:, C_CAUSAL:C_CAUSAL + P].unsqueeze(1).broadcast_to([P, 4, P]))
            for i in range(2):
                V.memset(V33[i][:, :, MD:MD + 1], 1.0)
            V.memset(neghalf[:], -0.5).then_inc(dve_const, 1)

            def statistics(src, bst_, mv_, ve_, s_bst, s_mv, s_ve, count, freed):
                if due(freed[1]):
                    dve.wait_ge(freed[0], freed[1])
                V.memset(wait_carrier[:], 0.0)
                V.bn_stats(bst_[:], src).then_inc(s_bst, 1)
                dve.wait_ge(s_bst, count)
                V.memset(wait_carrier[:], 0.0)
                V.bn_aggr(mv_[:], bst_[:]).then_inc(s_mv, 1)
                dve.wait_ge(s_mv, count)
                V.tensor_scalar_add(ve_[:], mv_[:, 1:2], EPS).then_inc(s_ve, 1)

            def query_statistics(b):
                statistics(x1[:, b, :], m_bst, m_mv, m_ve, mq_bst, mq_mv, mq_ve, b + 1, (mq_ready, b))

            def query(b, par):
                dve.wait_ge(mq_rstd, b + 1)
                if due(b - 1):
                    dve.wait_ge(mT_done, b - 1)
                V.tensor_scalar(qln[par][:], x1[:, b, :], m_mv[:, 0:1], m_rstd[:, 0:1], ALU.subtract, ALU.mult).then_inc(mq_ready, 1)

            def gate_inputs(b, par):
                dve.wait_ge(mg_done, b + 1)
                if due(b - 1):
                    dve.wait_ge(gg_ready, b - 1)
                V.tensor_tensor(gts[par][:], bY[:, 2 * MH:4 * MH], gbias[:], ALU.add).then_inc(gts_ready, 1)
                fg = gts[par][:, MH:2 * MH]
                dve.wait_ge(gts_ready, b + 1)
                if due(b):
                    dve.wait_ge(ef_ready, b)
                V.scalar_tensor_tensor(nf[:], fg, -1.0, fg, op0=ALU.mult, op1=ALU.min).then_inc(nf_ready, 1)

            def m_step(b, par):
                i, j, r = b - 1, b - 2, b - 3
                if live(b, NB):
                    dve.wait_ge(lf_ready, b + 1)
                    if due(b - 1):
                        dve.wait_ge(cs_done, b - 1)
                    V.scalar_tensor_tensor(logf[par][:], gts[par][:, MH:2 * MH], 0.0, lf[:], op0=ALU.min, op1=ALU.subtract).then_inc(logf_ready, 1)
                if live(i, NB):
                    bands = bSIM[:].rearrange("p r (h t) -> p (r h) t", h=4)
                    dve.wait_ge(gb_done, i + 1)
                    if due(i):
                        dve.wait_ge(dm_ready, i)
                    V.tensor_reduce(gmax[:], bands, axis=AX_X, op=ALU.max).then_inc(gmax_ready, 1)
                    dve.wait_ge(gmax_ready, i + 1)
                    if due(i):
                        dve.wait_ge(Dm_ready, i)
                    V.tensor_tensor(dm[:], bands, gmax[:].unsqueeze(2).broadcast_to([P, MH, P]), ALU.subtract).then_inc(dm_ready, 1)
                    dve.wait_ge(cs_ready, i + 1)
                    if due(i):
                        dve.wait_ge(en_ready, i)
                    V.tensor_tensor(mlog[:], csum[:], gmax[:], ALU.add).then_inc(mlog_ready, 1)
                if live(b, NB):
                    dve.wait_ge(cs_done, b + 1)
                    if due(b):
                        dve.wait_ge(gT_done, b)
                    V.tensor_tensor(gg[:], gts[par][:, 0:MH], bY[:, 0:MH], ALU.subtract).then_inc(gg_ready, 1)
                    if due(b):
                        dve.wait_ge(mlog_ready, b)
                    V.tensor_copy(csum[:], bY[:, 0:MH]).then_inc(cs_ready, 1)
                if live(r, NB):
                    dve.wait_ge(mh_rstd, r + 1)
                    V.tensor_scalar(hn[:], hm[:], h_mv[:, 0:1], h_rstd[:, 0:1], ALU.subtract, ALU.mult).then_inc(hn_ready, 1)
                    dve.wait_ge(hn_ready, r + 1)
                    V.tensor_tensor(hs[:], hn[:], mscale[:], ALU.mult).then_inc(hs_ready, 1)
                    dve.wait_ge(hs_ready, r + 1)
                    V.tensor_tensor(x1[:, r, :], x1[:, r, :], hs[:], ALU.add).then_inc(x1_ready, 1)
                if live(i, NB):
                    dve.wait_ge(Dm_ready, i + 1)
                    dve.wait_ge(mqk_done, i + 1)
                    if due(i - 1):
                        dve.wait_ge(CT_done, i - 1)
                    V.tensor_tensor(Cm[1 - par][:, 0:4].rearrange("p h t -> p (h t)"), bPT[:], Dm[:, 0:4].rearrange("p h t -> p (h t)"), ALU.mult)
                    V.tensor_tensor(Cm[1 - par][:, 4:8].rearrange("p h t -> p (h t)"), bTR[:], Dm[:, 4:8].rearrange("p h t -> p (h t)"), ALU.mult).then_inc(Cm_ready, 1)
                if live(r, NB):
                    dve.wait_ge(x1_ready, r + 1)
                    statistics(x1[:, r, :], f_bst, f_mv, f_ve, mf_bst, mf_mv, mf_ve, r + 1, (y_ready, r))
                if live(b + 2, NB):
                    query_statistics(b + 2)
                if live(j, NB):
                    hv = bV[:, 0:MH * (MD + 1)].rearrange("p (h d) -> p h d", h=MH)
                    dve.wait_ge(mpv_done, j + 1)
                    dve.wait_ge(en_ready, j + 1)
                    V.scalar_tensor_tensor(nneg[:].unsqueeze(2), hv[:, :, MD:MD + 1], -1.0, en[par][:].unsqueeze(2),
                                           op0=ALU.mult, op1=ALU.max).then_inc(nneg_ready, 1)
                    dve.wait_ge(nneg_ready, j + 1)
                    V.tensor_tensor(nrm[:].unsqueeze(2), hv[:, :, MD:MD + 1], nneg[:].unsqueeze(2), ALU.max).then_inc(nrm_ready, 1)
                    dve.wait_ge(nrm_ready, j + 1)
                    V.tensor_scalar_add(nrm2[:], nrm[:], M_EPS).then_inc(nrm2_ready, 1)
                    dve.wait_ge(nrm2_ready, j + 1)
                    if due(j):
                        dve.wait_ge(hm_ready, j)
                    V.reciprocal(nrec[:], nrm2[:]).then_inc(nrec_ready, 1)
                    dve.wait_ge(nrec_ready, j + 1)
                    if due(j):
                        dve.wait_ge(hn_ready, j)
                    V.tensor_tensor(hm[:].rearrange("p (h d) -> p h d", h=MH), hv[:, :, 0:MD],
                                    nrec[:].unsqueeze(2).broadcast_to([P, MH, MD]), ALU.mult).then_inc(hm_ready, 1)
                    dve.wait_ge(hm_ready, j + 1)
                    statistics(hm[:], h_bst, h_mv, h_ve, mh_bst, mh_mv, mh_ve, j + 1, (mh_rstd, j))
                if live(b + 1, NB):
                    gate_inputs(b + 1, 1 - par)
                if live(b + 2, NB):
                    query(b + 2, par)
                if live(r, NB):
                    dve.wait_ge(mf_rstd, r + 1)
                    V.tensor_scalar(y[:, r, :], x1[:, r, :], f_mv[:, 0:1], f_rstd[:, 0:1], ALU.subtract, ALU.mult).then_inc(y_ready, 1)

            query_statistics(0)
            query(0, 0)
            query_statistics(1)
            query(1, 1)
            gate_inputs(0, 0)
            dve.wait_ge(rest_in, 32)
            m_sweep(dve, m_step)
            dve.wait_ge(const_in, 16 * n_const)
            lower_xT(0, 0)
            sweep(dve, body)
            for i in range(4):
                q = slice(i * NB // 4, (i + 1) * NB // 4)
                dve.wait_ge(y_ready, NB * L + (i + 1) * NB // 4)
                V.tensor_tensor(y[:, q, :], y[:, q, :], x1[:, q, :], ALU.add).then_inc(res_ready, 1)

        @block.gpsimd
        def _(pool):
            T = nc.gpsimd.tensor_tensor

            def stage_y(G, par):
                pool.wait_ge(y_ready, G + 1)
                if due(G - 1):
                    pool.wait_ge(xt_done, G - 1)
                nc.gpsimd.tensor_copy(ycur[par][:], y[:, G % NB, :]).then_inc(ycur_ready, 1)

            def take_in(layer, g):
                pool.wait_ge(split_out, 16 * UNITS * (layer + 1))
                if due(layer):
                    pool.wait_ge(v_done, SLOTS * NPAIR * layer - GROUPS + g + 1)
                pool.dma_start(Wqkv[:, g * KC:(g + 1) * KC], split_dram[layer, g * KC:(g + 1) * KC].rearrange("c p h n -> p c h n")).then_inc(wqkv_in[g], 16)

            def body(n, split=True, refill=False):
                for k in range(SLOTS):
                    s = SLOTS * n + k
                    if k == 0 and live(n, NT):
                        layer = n // NPAIR
                        if due(SLOTS * n):
                            pool.wait_ge(u_ready, SLOTS * n)
                        gain = qk_gain[:, layer]
                        T(tabA[:], rotA, gain, ALU.mult)
                        T(tabB[:, :, 0:DH // 2], rotB[:, :, 0:DH // 2], gain[:, :, DH // 2:DH], ALU.mult)
                        T(tabB[:, :, DH // 2:DH], rotB[:, :, DH // 2:DH], gain[:, :, 0:DH // 2], ALU.mult).then_inc(tab_ready, 1)
                    if live(s, TS):
                        pool.wait_ge(ss_ready, s + 1)
                        if due(s):
                            pool.wait_ge(qn_ready, s)
                        T(rq[:], ss[:], neghalf[:], ALU.pow).then_inc(rq_ready, 1)
                        pool.wait_ge(qn_ready, s + 1)
                        pool.wait_ge(tab_ready, n + 1)
                        if due(s):
                            pool.wait_ge(u_ready, s)
                        for a in range(2):
                            src = qn[:, a * GF:(a + 1) * GF].rearrange("p (h d) -> p h d", h=HG)
                            dst = u2[:, a * GF:(a + 1) * GF].rearrange("p (h d) -> p h d", h=HG)
                            for lo, hi in ((0, DH // 2), (DH // 2, 0)):
                                last = T(dst[:, :, lo:lo + DH // 2], src[:, :, hi:hi + DH // 2],
                                         tabB[:, a:a + 1, lo:lo + DH // 2].broadcast_to([P, HG, DH // 2]), ALU.mult)
                        last.then_inc(u2_ready, 1)
                        pool.wait_ge(u2_ready, s + 1)
                        pool.wait_ge(u1_ready, s + 1)
                        if due(s - 1):
                            pool.wait_ge(tr_done, s - 1)
                        T(u[k % 2][:], u1[:], u2[:], ALU.add).then_inc(u_ready, 1)
                    if k in (2, 6):
                        G = 2 * n + (1 if k == 2 else 2)
                        if live(G, 2 * NT + 1):
                            stage_y(G, 1 if k == 2 else 0)
                    if k == 4 and live(n - 1, NT):
                        if due(n):
                            pool.wait_ge(ve_ready, n)
                        if due(n - 1):
                            pool.wait_ge(xn_ready, n - 1)
                        T(rstd[:], ve[:], neghalf[:, 0:2], ALU.pow).then_inc(rstd_ready, 1)
                    if refill and k >= GROUPS:
                        take_in(n // NPAIR + 1, k - GROUPS)

            pool.wait_ge(first_in, 16 * n_first)
            pool.wait_ge(dve_const, 3)

            def inverse_root(ve_, rstd_, s_ve, s_rstd, count, used):
                pool.wait_ge(s_ve, count)
                if due(count - 1):
                    pool.wait_ge(used, count - 1)
                T(rstd_[:], ve_[:], neghalf[:, 0:1], ALU.pow).then_inc(s_rstd, 1)

            def context_copy(b, par):
                if due(b - 1):
                    pool.wait_ge(mT_done, b - 1)
                if due(b - 1):
                    pool.wait_ge(v33_ready, b - 1)
                nc.gpsimd.tensor_copy(cst[par][:], y[:, b, :]).then_inc(mc_ready, 1)

            def masked_query(b, par):
                pool.wait_ge(mT_ready, b + 1)
                if due(b - 1):
                    pool.wait_ge(mqk_done, b - 1)
                for c in range(KC):
                    last = T(qm[par][:, 4 * c:4 * c + 4, :], qcT[par][:, c, :].unsqueeze(1).broadcast_to([P, 4, P]),
                             row_scale.unsqueeze(2).broadcast_to([P, 4, P]), ALU.mult)
                last.then_inc(qm_ready, 1)

            def m_step(b, par):
                if live(b + 1, NB):
                    masked_query(b + 1, 1 - par)
                j, r = b - 2, b - 3
                if live(r, NB):
                    inverse_root(f_ve, f_rstd, mf_ve, mf_rstd, r + 1, y_ready)
                if live(b + 2, NB):
                    inverse_root(m_ve, m_rstd, mq_ve, mq_rstd, b + 3, mq_ready)
                if live(j, NB):
                    inverse_root(h_ve, h_rstd, mh_ve, mh_rstd, j + 1, hn_ready)
                if live(b + 2, NB):
                    context_copy(b + 2, par)
                if isinstance(b, int) and b == NB + 1:
                    for g in range(GROUPS):
                        take_in(0, g)
                if par == 0:
                    w = b // 2
                    pool.wait_ge(hi_ready, w + 1)
                    if due(w):
                        pool.wait_ge(split_out, 16 * w)
                    T(unit_split[:, 1, :], unit[:], unit_split[:, 0, :], ALU.subtract).then_inc(lo_ready, 1)

            inverse_root(m_ve, m_rstd, mq_ve, mq_rstd, 1, mq_ready)
            context_copy(0, 0)
            inverse_root(m_ve, m_rstd, mq_ve, mq_rstd, 2, mq_ready)
            context_copy(1, 1)
            masked_query(0, 0)
            pool.wait_ge(rest_in, 32)
            m_sweep(pool, m_step)
            pool.wait_ge(const_in, 16 * n_const)
            stage_y(0, 0)
            sweep(pool, body)


def constants(S, D):
    import numpy as np
    f = np.float32
    t = np.arange(S, dtype=f)
    half = np.arange(0, DH, 2, dtype=f)
    inv_freq = (f(1.0) / f(10000.0) ** (half / f(DH))).astype(f)
    freqs = np.concatenate([t[:, None] * inv_freq[None, :]] * 2, -1).astype(f)
    base = (half + f(0.4 * DH)) / f(1.4 * DH)
    power = (t - S // 2) / f(DH // 2)
    scale = np.concatenate([(base[None, :] ** power[:, None])] * 2, -1).astype(f)
    cos, sin = np.cos(freqs), np.sin(freqs)
    sign = np.concatenate([-np.ones(DH // 2), np.ones(DH // 2)]).astype(f)
    i, j = np.arange(S)[:, None], np.arange(S)[None, :]
    pack = np.zeros((S, C_END), f)
    pack[:, C_IDENT:C_IDENT + S] = i == j
    pack[:, C_SHIFT:C_SHIFT + S] = j == i + 1
    pack[:, C_BAND:C_BAND + S] = np.where((j <= i) & (i <= j + DH), f(0), f(MASKED))
    pack[:, C_CAUSAL:C_CAUSAL + S] = np.where(j <= i, f(0), f(MASKED))
    pack[:, C_CUMSUM:C_CUMSUM + S] = i <= j
    for h in range(4):
        pack[MD * h:MD * (h + 1), C_ROWS + h] = f(1.0) / np.sqrt(f(MD))
    for h in range(MH):
        pack[h, C_PICK + h * P:C_PICK + (h + 1) * P] = 1
    pack[:, C_ROTA:C_ROTA + 2 * DH] = np.concatenate([cos * scale * f(QK_SCALE), cos / scale], 1)
    pack[:, C_ROTB:C_ROTB + 2 * DH] = np.concatenate([sin * sign * scale * f(QK_SCALE), sin * sign / scale], 1)
    return pack


def lay_out(w):
    import numpy as np
    a = {k: np.ascontiguousarray(v) for k, v in w.items()}
    L, D, _ = a['Wqkv'].shape
    kc, inner, gf = D // P, HEADS * DH, HG * DH
    f = a['W2'].shape[1]
    fc = -(-f // P)
    qkv = a['Wqkv'].reshape(L, kc, P, 3, GROUPS, gf)
    qkv = qkv.transpose(0, 4, 1, 2, 3, 5).reshape(L, GROUPS * kc, P, 3 * gf)
    wo = a['Wo'].reshape(L, inner // P, P, D).transpose(0, 2, 1, 3)
    whole = (fc - 1) * P
    w1 = np.zeros((L, D, 2 * fc - 1, P), a['W1'].dtype)
    halves = a['W1'].reshape(L, D, 2, f)
    w1[:, :, 0:2 * fc - 2] = halves[:, :, :, 0:whole].reshape(L, D, 2, fc - 1, P).transpose(0, 1, 3, 2, 4).reshape(L, D, 2 * fc - 2, P)
    w1[:, :, 2 * fc - 2, 0:f - whole] = halves[:, :, 0, whole:]
    w1[:, :, 2 * fc - 2, GATE_ROW:GATE_ROW + f - whole] = halves[:, :, 1, whole:]
    w1 = w1.reshape(L, kc, P, 2 * fc - 1, P).transpose(0, 2, 3, 1, 4)
    w2 = np.zeros((L, fc * P, D), a['W2'].dtype)
    w2[:, 0:f] = a['W2']
    w2 = w2.reshape(L, fc, P, D).transpose(0, 2, 1, 3)
    b1 = np.zeros((L, 2, fc * P), a['b1'].dtype)
    b1[:, :, 0:f] = a['b1'].reshape(L, 2, f)
    b1[:, 1, whole + GATE_ROW:whole + GATE_ROW + f - whole] = b1[:, 1, whole:f].copy()
    b1 = b1.reshape(L, 2, fc, P).transpose(3, 0, 1, 2)
    gates = np.stack([a['igate_w'], a['fgate_w']]).reshape(2 * MH, 3 * kc, P).transpose(2, 1, 0)
    gate_b = np.stack([a['igate_b'], a['fgate_b']]).reshape(1, 2 * MH)
    g, b = (a[k].reshape(L, kc, P).transpose(2, 0, 1) for k in ('ln_g', 'ln_b'))
    return dict(gate_w=gates, gate_b=gate_b, mln_scale=a['ln_scale'].reshape(1, D), wqkv=qkv, q_scale=a['q_scale'], k_scale=a['k_scale'], wo=wo, ln_g=g, ln_b=b, w1=w1, b1=b1, w2=w2,
                b2=a['b2'])


def kernel(**inputs):
    import numpy as _np
    import concourse.bacc as _bacc
    from concourse import mybir as _mybir
    from concourse.bass_utils import run_bass_kernel_spmd as _run

    nc = _bacc.Bacc("TRN2", target_bir_lowering=False, num_devices=1)
    arrays, args = {}, {}
    x = inputs['x']
    w = dict(x=x, ctxt=inputs['ctx_1024'], consts=constants(*x.shape[1:]))
    w.update(lay_out({k.split('_', 2)[2]: v for k, v in inputs.items() if k.startswith('L0_')}))
    for name, a in w.items():
        a = _np.ascontiguousarray(a)
        arrays[f"in_{name}_dram"] = a
        args[name] = nc.dram_tensor(f"in_{name}_dram", a.shape, _mybir.dt.from_np(a.dtype), kind="ExternalInput").ap()
    shape = x.shape
    out = nc.dram_tensor("out_dram", shape, _mybir.dt.float32, kind="ExternalOutput").ap()
    program(nc, args['x'], args['ctxt'], args['gate_w'], args['gate_b'], args['mln_scale'], args['consts'], args['wqkv'], args['q_scale'], args['k_scale'], args['wo'], args['ln_g'],
            args['ln_b'], args['w1'], args['b1'], args['w2'], args['b2'], inputs['L0_ffn_W2'].shape[1], out)
    r = _run(nc, [arrays], core_ids=[0])
    return r.results[0]["out_dram"]
```
